# Optimizing a Trainium2 kernel written in Bass

```python
import numpy as np
import jax
import jax.numpy as jnp

def _softmax(x, axis=-1):
    return jax.nn.softmax(x, axis=axis)

def _gelu(x):
    return jax.nn.gelu(x, approximate=True)

def _silu(x):
    return jax.nn.silu(x)

def _sigmoid(x):
    return jax.nn.sigmoid(x)

def _layernorm(x, axis=-1, eps=1e-05):
    m = jnp.mean(x, axis=axis, keepdims=True)
    v = jnp.var(x, axis=axis, keepdims=True)
    return (x - m) / jnp.sqrt(v + eps)

def _scatter_add(tgt, idx, src, axis=0):
    return tgt.at[idx].add(src)

def _segment_sum(src, seg, n):
    return jax.ops.segment_sum(src, seg, n)
kernel_name = 'mk_gnn_resnorm_d4_gnn_r32_a75adf'

def setup_inputs(seed: int=0):
    np.random.seed(seed)
    _w = jnp.asarray

    def _rec_inputs():
        import jax
        import jax.numpy as jnp
        _gk = jax.random.key(seed)
        x = -6.415e-05 + 1 * jax.random.normal(jax.random.fold_in(_gk, 1), (625, 512), jnp.float32)
        src = jax.random.randint(jax.random.fold_in(_gk, 2), (10000,), 0, 625, jnp.int32)
        dst = jnp.minimum((625 * jax.random.uniform(jax.random.fold_in(_gk, 3), (10000,)) ** 2.0).astype(jnp.int32), 19999)
        _o = jnp.argsort(dst, stable=True)
        src = src[_o]
        dst = dst[_o]
        edge_type_3 = jax.random.randint(jax.random.fold_in(_gk, 13), (10000,), 0, 3, jnp.int32)
        edge_weight1 = -0.00598325 + 0.997157 * jax.random.normal(jax.random.fold_in(_gk, 14), (10000, 1), jnp.float32)
        node_type_3 = jax.random.randint(jax.random.fold_in(_gk, 15), (625,), 0, 3, jnp.int32)
        return (x, src, dst, edge_type_3, edge_weight1, node_type_3)
    x, src, dst, edge_type_3, edge_weight1, node_type_3 = _rec_inputs()

    def _L0_gnn_setup():
        import jax, jax.numpy as jnp
        import numpy as np
        N_NODES = 625
        N_EDGES = 150000
        D_IN = 512
        D_OUT = 512
        N_REL = 3
        N_NT = 3
        key = jax.random.key(seed)
        ks = jax.random.split(key, 8)
        x = jax.random.normal(ks[0], (N_NODES, D_IN), dtype=jnp.float32)
        W_rel = jax.random.normal(ks[1], (N_REL, D_IN, D_OUT), dtype=jnp.float32) * 0.02
        b_rel = jnp.zeros((N_REL, D_OUT), dtype=jnp.float32)
        W_self = jax.random.normal(ks[2], (N_NT, D_IN, D_OUT), dtype=jnp.float32) * 0.02
        b_self = jnp.zeros((N_NT, D_OUT), dtype=jnp.float32)
        edge_src = jax.random.randint(ks[3], (N_EDGES,), 0, N_NODES, dtype=jnp.int32)
        edge_dst = jax.random.randint(ks[4], (N_EDGES,), 0, N_NODES, dtype=jnp.int32)
        edge_type = jax.random.randint(ks[5], (N_EDGES,), 0, N_REL, dtype=jnp.int32)
        node_type = jax.random.randint(ks[6], (N_NODES,), 0, N_NT, dtype=jnp.int32)
        return {'x': x, 'W_rel': W_rel, 'b_rel': b_rel, 'W_self': W_self, 'b_self': b_self, 'edge_src': edge_src, 'edge_dst': edge_dst, 'edge_type': edge_type, 'node_type': node_type}
    _L0_gnn_all = _L0_gnn_setup()
    _L0_gnn_in = {k: v for k, v in _L0_gnn_all.items() if k in ('W_rel', 'b_rel', 'W_self', 'b_self')}
    del _L0_gnn_all

    def _L1_gnn_setup():
        import jax, jax.numpy as jnp
        import numpy as np
        N_NODES = 3125
        N_EDGES = 25600
        D = 512
        L = 3
        LN_EPS = 1e-05
        key = jax.random.key(seed)
        ks = jax.random.split(key, 8)
        x = jax.random.normal(ks[0], (N_NODES, D), dtype=jnp.float32)
        edge_index = jax.random.randint(ks[1], (2, N_EDGES), 0, N_NODES, dtype=jnp.int32)
        scale = 1.0 / np.sqrt(D)
        W_l = jax.random.normal(ks[2], (L, D, D), dtype=jnp.float32) * scale
        W_r = jax.random.normal(ks[3], (L, D, D), dtype=jnp.float32) * scale
        b = jax.random.normal(ks[4], (L, D), dtype=jnp.float32) * 0.01
        ln_g = jnp.ones((L, D), dtype=jnp.float32)
        ln_b = jnp.zeros((L, D), dtype=jnp.float32)
        return {'x': x, 'edge_index': edge_index, 'W_l': W_l, 'W_r': W_r, 'b': b, 'ln_g': ln_g, 'ln_b': ln_b}
    _L1_gnn_all = _L1_gnn_setup()
    _L1_gnn_in = {k: v for k, v in _L1_gnn_all.items() if k in ('W_l', 'W_r', 'b', 'ln_g', 'ln_b')}
    del _L1_gnn_all

    def _L2_gnn_setup():
        import jax, jax.numpy as jnp
        import numpy as np
        N, D, E, L = (625, 512, 5000, 4)
        BN_EPS = 1e-05

        def _gine_layer(x, src, dst, edge_attr, eps, We, be, W1, b1, gamma, beta, W2, b2):
            e = edge_attr @ We + be
            m = jax.nn.relu(x[src] + e)
            agg = jax.ops.segment_sum(m, dst, num_segments=x.shape[0])
            h = ((1.0 + eps) * x + agg) @ W1 + b1
            mu = jnp.mean(h, axis=0)
            var = jnp.mean(jnp.square(h - mu), axis=0)
            h = (h - mu) * jax.lax.rsqrt(var + BN_EPS) * gamma + beta
            h = jax.nn.relu(h)
            return jax.nn.relu(h @ W2 + b2)
        key = jax.random.key(seed)
        ks = jax.random.split(key, 10)
        x = jax.random.normal(ks[0], (N, D), dtype=jnp.float32)
        edge_index = jax.random.randint(ks[1], (2, E), 0, N, dtype=jnp.int64)
        edge_attr = jax.random.normal(ks[2], (E, 1), dtype=jnp.float32)
        s1 = 1.0 / np.sqrt(D)
        params = {'eps': jnp.zeros((L,), jnp.float32), 'We': jax.random.normal(ks[3], (L, 1, D), jnp.float32) * 1.0, 'be': jnp.zeros((L, D), jnp.float32), 'W1': jax.random.normal(ks[4], (L, D, D), jnp.float32) * s1, 'b1': jnp.zeros((L, D), jnp.float32), 'gamma': jnp.ones((L, D), jnp.float32), 'beta': jnp.zeros((L, D), jnp.float32), 'W2': jax.random.normal(ks[5], (L, D, D), jnp.float32) * s1, 'b2': jnp.zeros((L, D), jnp.float32)}
        return {'x': x, 'edge_index': edge_index, 'edge_attr': edge_attr, **params}
    _L2_gnn_all = _L2_gnn_setup()
    _L2_gnn_in = {k: v for k, v in _L2_gnn_all.items() if k in ('eps', 'We', 'be', 'W1', 'b1', 'gamma', 'beta', 'W2', 'b2')}
    del _L2_gnn_all

    def _L3_gnn_setup():
        import jax, jax.numpy as jnp
        import numpy as np
        N_NODES = 10000
        N_EDGES = 5000
        D_IN = 512
        D_OUT = 512
        key = jax.random.key(seed)
        k_x, k_e, k_wl, k_wr = jax.random.split(key, 4)
        x = jax.random.normal(k_x, (N_NODES, D_IN), dtype=jnp.float32)
        edge_index = jax.random.randint(k_e, (2, N_EDGES), 0, N_NODES, dtype=jnp.int64)
        scale = 1.0 / np.sqrt(D_IN)
        W_l = jax.random.normal(k_wl, (D_IN, D_OUT), dtype=jnp.float32) * scale
        W_r = jax.random.normal(k_wr, (D_IN, D_OUT), dtype=jnp.float32) * scale
        b = jnp.zeros((D_OUT,), dtype=jnp.float32)
        return {'x': x, 'edge_index': edge_index, 'W_l': W_l, 'W_r': W_r, 'b': b}
    _L3_gnn_all = _L3_gnn_setup()
    _L3_gnn_in = {k: v for k, v in _L3_gnn_all.items() if k in ('W_l', 'W_r', 'b')}
    del _L3_gnn_all
    return {'x': x, 'src': src, 'dst': dst, 'edge_type_3': edge_type_3, 'edge_weight1': edge_weight1, 'node_type_3': node_type_3, 'L0_gnn_W_rel': _L0_gnn_in['W_rel'], 'L0_gnn_b_rel': _L0_gnn_in['b_rel'], 'L0_gnn_W_self': _L0_gnn_in['W_self'], 'L0_gnn_b_self': _L0_gnn_in['b_self'], 'L1_gnn_W_l': _L1_gnn_in['W_l'], 'L1_gnn_W_r': _L1_gnn_in['W_r'], 'L1_gnn_b': _L1_gnn_in['b'], 'L1_gnn_ln_g': _L1_gnn_in['ln_g'], 'L1_gnn_ln_b': _L1_gnn_in['ln_b'], 'L2_gnn_eps': _L2_gnn_in['eps'], 'L2_gnn_We': _L2_gnn_in['We'], 'L2_gnn_be': _L2_gnn_in['be'], 'L2_gnn_W1': _L2_gnn_in['W1'], 'L2_gnn_b1': _L2_gnn_in['b1'], 'L2_gnn_gamma': _L2_gnn_in['gamma'], 'L2_gnn_beta': _L2_gnn_in['beta'], 'L2_gnn_W2': _L2_gnn_in['W2'], 'L2_gnn_b2': _L2_gnn_in['b2'], 'L3_gnn_W_l': _L3_gnn_in['W_l'], 'L3_gnn_W_r': _L3_gnn_in['W_r'], 'L3_gnn_b': _L3_gnn_in['b']}

def reference(x, src, dst, edge_type_3, edge_weight1, node_type_3, L0_gnn_W_rel, L0_gnn_b_rel, L0_gnn_W_self, L0_gnn_b_self, L1_gnn_W_l, L1_gnn_W_r, L1_gnn_b, L1_gnn_ln_g, L1_gnn_ln_b, L2_gnn_eps, L2_gnn_We, L2_gnn_be, L2_gnn_W1, L2_gnn_b1, L2_gnn_gamma, L2_gnn_beta, L2_gnn_W2, L2_gnn_b2, L3_gnn_W_l, L3_gnn_W_r, L3_gnn_b):
    import jax
    import jax.numpy as jnp

    def _L0_gnn_ref(x, W_rel, b_rel, W_self, b_self, edge_src, edge_dst, edge_type, node_type):
        import jax, jax.numpy as jnp
        import numpy as np
        N_NODES = 625
        N_EDGES = 150000
        D_IN = 512
        D_OUT = 512
        N_REL = 3
        N_NT = 3
        xr = jnp.einsum('nd,rde->rne', x, W_rel)
        msg = xr[edge_type, edge_src] + b_rel[edge_type]
        agg = jax.ops.segment_sum(msg, edge_dst, num_segments=N_NODES)
        xs = jnp.einsum('nd,tde->tne', x, W_self)
        h_self = xs[node_type, jnp.arange(N_NODES)] + b_self[node_type]
        return jax.nn.relu(h_self + agg)

    def _L1_gnn_ref(x, edge_index, W_l, W_r, b, ln_g, ln_b):
        import jax, jax.numpy as jnp
        import numpy as np
        N_NODES = 3125
        N_EDGES = 25600
        D = 512
        L = 3
        LN_EPS = 1e-05
        src = edge_index[0]
        tgt = edge_index[1]
        n = x.shape[0]
        cnt = jax.ops.segment_sum(jnp.ones((src.shape[0],), x.dtype), tgt, num_segments=n)
        inv_cnt = (1.0 / jnp.maximum(cnt, 1.0))[:, None]
        for i in range(W_l.shape[0]):
            x_in = x
            agg = jax.ops.segment_sum(x[src], tgt, num_segments=n) * inv_cnt
            h = agg @ W_l[i].T + x @ W_r[i].T + b[i]
            mu = jnp.mean(h, axis=-1, keepdims=True)
            var = jnp.mean(jnp.square(h - mu), axis=-1, keepdims=True)
            h = (h - mu) * jax.lax.rsqrt(var + LN_EPS) * ln_g[i] + ln_b[i]
            h = jax.nn.relu(h)
            x = h + x_in
        return x

    def _L2_gnn_ref(x, edge_index, edge_attr, eps, We, be, W1, b1, gamma, beta, W2, b2):
        import jax, jax.numpy as jnp
        import numpy as np
        N, D, E, L = (625, 512, 5000, 4)
        BN_EPS = 1e-05

        def _gine_layer(x, src, dst, edge_attr, eps, We, be, W1, b1, gamma, beta, W2, b2):
            e = edge_attr @ We + be
            m = jax.nn.relu(x[src] + e)
            agg = jax.ops.segment_sum(m, dst, num_segments=x.shape[0])
            h = ((1.0 + eps) * x + agg) @ W1 + b1
            mu = jnp.mean(h, axis=0)
            var = jnp.mean(jnp.square(h - mu), axis=0)
            h = (h - mu) * jax.lax.rsqrt(var + BN_EPS) * gamma + beta
            h = jax.nn.relu(h)
            return jax.nn.relu(h @ W2 + b2)
        src, dst = (edge_index[0], edge_index[1])
        for l in range(L):
            x = _gine_layer(x, src, dst, edge_attr, eps[l], We[l], be[l], W1[l], b1[l], gamma[l], beta[l], W2[l], b2[l])
        return x

    def _L3_gnn_ref(x, edge_index, W_l, W_r, b):
        import jax, jax.numpy as jnp
        import numpy as np
        N_NODES = 10000
        N_EDGES = 5000
        D_IN = 512
        D_OUT = 512
        src = edge_index[0]
        dst = edge_index[1]
        n = x.shape[0]
        msg = x[src]
        agg = jax.ops.segment_sum(msg, dst, num_segments=n)
        deg = jax.ops.segment_sum(jnp.ones((src.shape[0],), x.dtype), dst, num_segments=n)
        mean = agg / jnp.maximum(deg, 1.0)[:, None]
        h = mean @ W_l + b + x @ W_r
        return h * jax.nn.sigmoid(h)
    edge_index = jnp.stack([src, dst])
    x = _layernorm(x + _L0_gnn_ref(x, L0_gnn_W_rel, L0_gnn_b_rel, L0_gnn_W_self, L0_gnn_b_self, src, dst, edge_type_3, node_type_3), axis=-1)
    x = _layernorm(x + _L1_gnn_ref(x, edge_index, L1_gnn_W_l, L1_gnn_W_r, L1_gnn_b, L1_gnn_ln_g, L1_gnn_ln_b), axis=-1)
    x = _layernorm(x + _L2_gnn_ref(x, edge_index, edge_weight1, L2_gnn_eps, L2_gnn_We, L2_gnn_be, L2_gnn_W1, L2_gnn_b1, L2_gnn_gamma, L2_gnn_beta, L2_gnn_W2, L2_gnn_b2), axis=-1)
    x = _layernorm(x + _L3_gnn_ref(x, edge_index, L3_gnn_W_l, L3_gnn_W_r, L3_gnn_b), axis=-1)
    return x

_drawn_inputs = setup_inputs


def setup_inputs(seed=0):
    import zlib

    import numpy as np

    out = dict(_drawn_inputs(seed))
    spreads = {'L0_gnn_b_rel': (0.0, 0.1),
     'L0_gnn_b_self': (0.0, 0.1),
     'L1_gnn_ln_g': (1.0, 0.2),
     'L1_gnn_ln_b': (0.0, 0.1),
     'L2_gnn_eps': (0.0, 2.0),
     'L2_gnn_be': (0.0, 0.1),
     'L2_gnn_b1': (0.0, 2.0),
     'L2_gnn_gamma': (1.0, 0.2),
     'L2_gnn_beta': (0.0, 0.1),
     'L2_gnn_b2': (0.0, 0.1),
     'L3_gnn_b': (0.0, 0.1)}
    factors = {'L1_gnn_b': 8.0}
    for name, (base, spread) in spreads.items():
        noise = np.random.default_rng([zlib.crc32(name.encode()), seed]).standard_normal(out[name].shape)
        drawn = base * np.exp(spread * noise) if base else spread * noise
        out[name] = jnp.asarray(drawn.astype(out[name].dtype))
    for name, factor in factors.items():
        out[name] = (out[name] * factor).astype(out[name].dtype)
    return out
```

```python
from contextlib import ExitStack

import numpy as np

import concourse.bass as bass
from concourse import mybir

ALU = mybir.AluOpType
ACT = mybir.ActivationFunctionType
AX_X = mybir.AxisListType.X
F32 = mybir.dt.float32
F16 = mybir.dt.float16
BF16 = mybir.dt.bfloat16
I32 = mybir.dt.int32

P = 128
N = 625
D = 512
E = 10000
NT = -(-N // P)
NP = NT * P
LAST = N - (NT - 1) * P
KT = D // P
HALF = NP // 2
EP = 125
EC = E // EP
RING = 12
GRP = 4
TE = -(-((E - NT) // P + NT) // RING) * RING
PASSES = TE // RING
ZR = 4
RECW = 5
SCG = 8
LN_EPS = 1e-5
NREL = 3
NL1 = 3
NL2 = 4


class Chain:

    def __init__(self, eng, sem):
        self.eng, self.sem, self.n, self.reg = eng, sem, 0, None

    def link(self, ins):
        self.n += 1
        ins.then_inc(self.sem, 1)
        self.eng.wait_ge(self.sem, self.n if self.reg is None else self.reg + self.n)

    def enter(self, reg_part):
        self.reg, self.start = reg_part, self.n

    def leave(self, per, times):
        assert self.n - self.start == per, (self.n - self.start, per)
        self.reg = None
        self.n = self.start + per * times


def build(nc, x, src, dst, etype, ew, ntype, w_rel, b_rel, w_self, b_self, wlt, wrt, b1_l1, ln_g, ln_b,
          eps, we, be, w1, w2, cols, b2, w3l, w3r, b3, out):
    rec_d = nc.dram_tensor("edge_records", (P * TE, 4), I32).ap()
    xr_d = nc.dram_tensor("rel_rows", (NREL * NP, D), F32).ap()
    xg_d = nc.dram_tensor("gine_rows", (NP, D), F32).ap()

    with ExitStack() as ctx:
        def sb(name, shape, dt=F32):
            return ctx.enter_context(nc.sbuf_tensor(name, shape, dt))

        def sem(name):
            return ctx.enter_context(nc.semaphore(name))

        B = sb("block_in", [P, NT, D])
        X = sb("x_cur", [P, NT, D])
        H = sb("work", [P, NT, D])
        XT = sb("xT", [P, KT, NP])
        TH = sb("t_work", [P, 2, KT, NP])
        GT, HT = TH[:, 0], TH[:, 1]
        AN = TH[:, :, :, :].rearrange("p a k n -> p (a k n)")[:, 0:NT * NP].rearrange("p (t s) -> p t s", t=NT)
        AT = sb("adjT", [P, NT, NP])
        W = [sb(f"w{i}", [P, KT, D]) for i in range(4)]
        ROW = [sb(f"row{i}", [P, D]) for i in range(6)]
        G = [sb(f"gathered{i}", [P, D]) for i in range(RING)]
        Z = [sb(f"edge_rows{i}", [P, D]) for i in range(ZR)]
        S = [sb(f"onehot_dst{i}", [P, P]) for i in range(ZR)]
        SB = [sb(f"onehot_dst_b{i}", [P, P], BF16) for i in range(ZR)]
        OS = [sb(f"onehot_src{i}", [P, NP], BF16) for i in range(ZR)]
        RS = sb("records", [P, TE, 4], I32)
        IDX = sb("gather_idx", [P, RING], I32)
        srcf = sb("srcf", [P, TE])
        tile_of = sb("bucket_of_tile", [1, TE], I32)
        e_dst = sb("e_dst", [EP, EC], I32)
        e_src = sb("e_src", [EP, EC], I32)
        e_typ = sb("e_typ", [EP, EC], I32)
        e_w = sb("e_w", [EP, EC])
        REC = sb("rec_sb", [EP, EC, RECW], I32)
        STG = sb("rec_stage", [EP, 2, SCG, RECW], I32)
        PAD = sb("rec_pad", [P, TE, 4], I32)
        ti = sb("ti", [EP, EC], I32)
        ti2 = sb("ti2", [EP, EC], I32)
        bk = sb("bk", [EP, EC])
        oh = sb("oh", [EP, NT, EC])
        run = sb("run", [EP, NT, EC])
        one80 = sb("one80", [EP, EC])
        slot = sb("slot", [EP, EC])
        tri = sb("tri", [EP, P])
        ones = sb("ones", [EP, P])
        base = sb("base", [P, 4, NT])
        basei = sb("basei", [P, NT], I32)
        tf = sb("tf", [1, 2, TE])
        iota_f = sb("iota_f", [P, P])
        iota_h = sb("iota_h", [P, NP], F16)
        iota_t = sb("iota_t", [1, TE])
        ident = sb("ident", [P, P])
        zero = sb("zero", [P, D], BF16)
        epst = sb("epst", [P, 1])
        nti = sb("nti", [P, NT], I32)
        mask = sb("mask", [P, NREL, NT])
        eps1 = sb("eps1", [P, NL2])
        colt = sb("colt", [P, 3, NL2, KT])
        lcol = sb("lcol", [P, 3, KT])
        st = sb("st", [P, NT, 2, 6])
        msc = sb("msc", [P, KT])
        mv = sb("mv", [P, NT, 2])
        sd = sb("sd", [P, NT])
        rstd = sb("rstd", [P, NT])
        deg = sb("deg", [P, 2, NT])
        sc = sb("sc", [P, 2, KT])
        ps = ctx.enter_context(nc.psum_tensor("ps", [P, 8, D], F32))
        ps_tail = ps[:, 5:7, :].rearrange("p a n -> p (a n)")

        consts = sem("consts")
        tri0 = sem("tri0")
        edges_in = sem("edges_in")
        small_in = sem("small_in")
        x_in = sem("x_in")
        tail_clear = sem("tail_clear")
        pad_made = sem("pad_made")
        pad_out = sem("pad_out")
        w_in = [sem(f"w{i}_in") for i in range(4)]
        row_in = [sem(f"row{i}_in") for i in range(6)]
        dve = sem("dve_chain")
        dve_step = sem("dve_step")
        lcol_made = sem("lcol_made")
        tot_made = sem("tot_made")
        pre_made = sem("pre_made")
        pre_read = sem("pre_read")
        rec_made = sem("rec_made")
        staged = sem("rec_staged")
        scat = [sem(f"scattered{i}") for i in range(2)]
        sp_step = sem("sp_step")
        pool_step = sem("pool_step")
        rec_in = sem("rec_in")
        rec_ok = sem("rec_ok")
        bucket_made = sem("bucket_made")
        oh_made = sem("onehots_made")
        oh_used = sem("onehots_used")
        cnt_done = sem("counts_done")
        cnt_out = sem("counts_out")
        adj_made = sem("adj_made")
        adj_tr = sem("adj_tr")
        adj_out = sem("adj_out")
        tr_done = sem("tr_done")
        tr_out = sem("tr_out")
        prod_done = sem("prod_done")
        prod_out = sem("prod_out")
        xr_out = sem("xr_out")
        ring_free = sem("ring_free")
        idx_made = sem("idx_made")
        gath = [sem(f"gath{i}") for i in range(RING)]
        s_made = sem("onehot_made")
        z_free = sem("z_free")
        z_made = sem("z_relu")
        acc_open = sem("acc_open")
        acc_done = sem("acc_done")
        x_made = sem("x_made")
        b_made = sem("b_made")
        ln_var = sem("ln_var")
        ln_sd = sem("ln_sd")
        agg_done = sem("agg_done")
        agg_out = sem("agg_out")
        we_ok = sem("we_ok")
        xp_made = sem("xp_made")
        xg_out = sem("xg_out")
        g_made = sem("g_made")
        ht_done = sem("ht_done")
        ht_raw = sem("ht_raw")
        bn_var = sem("bn_var")
        bn_sd = sem("bn_sd")
        bn_sc = sem("bn_sc")
        ht_out = sem("ht_out")
        sg_in = sem("sg_in")
        sg_out = sem("sg_out")
        o_made = sem("o_made")
        o_out = sem("o_out")
        we_psum = ps[:, 5, :]

        xv = [x[n * P:min(N, n * P + P), :] for n in range(NT)]
        block = ctx.enter_context(nc.Block())

        @block.sync
        def _(sp):
            def w_load(i, w):
                sp.dma_start(W[i][:, :, :], w.rearrange("(k p) n -> p k n", p=P)).then_inc(w_in[i], 16)

            def row_load(i, r):
                sp.dma_start(ROW[i][:, :], r.broadcast_to([P, D])).then_inc(row_in[i], 16)

            for t, d in ((e_dst, dst), (e_src, src), (e_typ, etype), (e_w, ew)):
                sp.dma_start(t[:, :], d).then_inc(edges_in, 16)
            for n in range(NT - 1):
                sp.dma_start(B[:, n, :], xv[n]).then_inc(x_in, 16)
            sp.wait_ge(tail_clear, 1)
            sp.dma_start(B[0:LAST, NT - 1, :], xv[NT - 1]).then_inc(x_in, 16)
            w_load(0, w_rel[0])
            sp.dma_start(nti[:, :], ntype).then_inc(small_in, 16)
            sp.dma_start(eps1[:, :], eps.broadcast_to([P, NL2])).then_inc(small_in, 16)
            sp.dma_start(colt[:, :, :, :], cols).then_inc(small_in, 16)
            sp.wait_ge(pad_made, 1)
            sp.dma_start(rec_d.rearrange("(p t) r -> p t r", p=P), PAD[:, :, :]).then_inc(pad_out, 16)
            for r in range(NREL):
                row_load(r, b_rel[r:r + 1, :])
                row_load(3 + r, b_self[r:r + 1, :])
            w_load(1, w_rel[1])
            w_load(2, w_rel[2])
            w_load(3, w_self[0])
            for q in range(NREL * NT):
                sp.wait_ge(prod_out, q + 1)
                r, n = divmod(q, NT)
                rows = G[q] if q < RING else X[:, q - RING]
                sp.dma_start(xr_d[r * NP + n * P:r * NP + (n + 1) * P, :], rows[:, :] if q < RING else rows)\
                    .then_inc(xr_out, 16)
                if q == NT:
                    w_load(0, w_self[1])
                if q == 2 * NT:
                    w_load(1, w_self[2])
            for hf in range(2):
                sp.wait_ge(scat[hf], 16 * (E // EP) // 2)
            sp.dma_start(RS[:, :, :], rec_d.rearrange("(p t) r -> p t r", p=P)).then_inc(rec_in, 16)

            with sp.Fori(0, NL1) as l:
                sp.wait_ge(prod_done, 2 * NREL * NT + l * NT)
                sp.sem_inc(sp_step, 1)
                sp.dma_start(W[2][:, :, :], wlt[bass.ds(l, 1), :, :].rearrange("o (k p) n -> p (o k) n", p=P))\
                    .then_inc(w_in[2], 16)
                sp.dma_start(W[3][:, :, :], wrt[bass.ds(l, 1), :, :].rearrange("o (k p) n -> p (o k) n", p=P))\
                    .then_inc(w_in[3], 16)
                sp.wait_ge(x_made, l * NT + NT)
                sp.sem_inc(sp_step, 1)
                for i, r in ((0, b1_l1), (1, ln_g), (2, ln_b)):
                    sp.dma_start(ROW[i][:, :], r[bass.ds(l, 1), :].broadcast_to([P, D])).then_inc(row_in[i], 16)
            row_load(3, we[0:1, :])
            row_load(4, be[0:1, :])
            with sp.Fori(0, NL2) as l:
                for n in range(NT):
                    sp.wait_ge(xp_made, l * NT + n + 1)
                    sp.dma_start(xg_d[n * P:(n + 1) * P, :], H[:, n, :]).then_inc(xg_out, 16)
                sp.dma_start(W[0][:, :, :], w1[bass.ds(l, 1), :, :].rearrange("o (k p) n -> p (o k) n", p=P))\
                    .then_inc(w_in[0], 16)
                sp.dma_start(W[1][:, :, :], w2[bass.ds(l, 1), :, :].rearrange("o (k p) n -> p (o k) n", p=P))\
                    .then_inc(w_in[1], 16)
                sp.dma_start(ROW[5][:, :], b2[bass.ds(l, 1), :].broadcast_to([P, D])).then_inc(row_in[5], 16)
                sp.dma_start(ROW[4][:, :], be[bass.ds(l + 1, 1), :].broadcast_to([P, D])).then_inc(row_in[4], 16)
                sp.wait_ge(we_ok, l + 1)
                sp.sem_inc(sp_step, 1)
                sp.dma_start(ROW[3][:, :], we[bass.ds(l + 1, 1), :].broadcast_to([P, D])).then_inc(row_in[3], 16)
            w_load(2, w3l)
            w_load(3, w3r)
            row_load(0, b3)
            for n in range(NT):
                sp.wait_ge(o_made, n + 1)
                rows = P if n < NT - 1 else LAST
                sp.dma_start(out[n * P:n * P + rows, :], H[0:rows, n, :]).then_inc(o_out, 16)
            sp.wait_ge(o_out, 16 * NT)
            sp.wait_ge(row_in[3], 16 * (NL2 + 2))
            sp.wait_ge(row_in[4], 16 * (NL2 + 2))

        @block.gpsimd
        def _(gp):
            gp.memset(tri[:, :], 1.0).then_inc(tri0, 1)
            gp.memset(ident[:, :], 0.0).then_inc(tri0, 1)
            gp.memset(ones[:, :], 1.0).then_inc(consts, 1)
            gp.wait_ge(tri0, 2)
            gp.affine_select(out=tri[:, :], in_=tri[:, :], compare_op=ALU.is_gt, fill=0.0, base=0,
                             pattern=[[1, P]], channel_multiplier=-1).then_inc(consts, 1)
            gp.affine_select(out=ident[:, :], in_=ident[:, :], compare_op=ALU.not_equal, fill=1.0, base=0,
                             pattern=[[-1, P]], channel_multiplier=1).then_inc(consts, 1)
            gp.iota(iota_f[:, :], [[1, P]], base=0, channel_multiplier=0,
                    allow_small_or_imprecise_dtypes=True).then_inc(consts, 1)
            gp.iota(iota_h[:, :], [[1, NP]], base=0, channel_multiplier=0,
                    allow_small_or_imprecise_dtypes=True).then_inc(consts, 1)
            gp.iota(iota_t[:, :], [[1, TE]], base=0, channel_multiplier=0,
                    allow_small_or_imprecise_dtypes=True).then_inc(consts, 1)

            gp.wait_ge(pad_out, 16)
            gp.wait_ge(rec_made, 1)

            def scatter(hf, group):
                gp.tensor_copy(STG[:, hf, :, :], REC[:, bass.ds(group * SCG, SCG), :]).then_inc(staged, 1)
                gp.wait_ge(staged, group + 1)
                gp.sem_inc(pool_step, 1)
                for k in range(SCG):
                    gp.indirect_dma_start(
                        rec_d, bass.IndirectOffsetOnAxis(ap=STG[:, hf, k, 4:5], axis=0),
                        STG[:, hf, k, 0:4], None).then_inc(scat[hf], 16)

            for hf in range(2):
                scatter(hf, hf)
            with gp.Fori(1, EC // (2 * SCG)) as i:
                for hf in range(2):
                    gp.wait_ge(scat[hf], i * (16 * SCG))
                    gp.sem_inc(pool_step, 1)
                    scatter(hf, 2 * i + hf)

            def gather(passes_before, i, table, column):
                for q in range(RING // GRP):
                    gp.wait_ge(ring_free, (i + passes_before) * RING + GRP * (q + 1))
                    gp.sem_inc(pool_step, 1)
                    gp.tensor_copy(IDX[:, q * GRP:(q + 1) * GRP],
                                   RS[:, bass.ds(i * RING + q * GRP, GRP), column]).then_inc(idx_made, 1)
                    gp.wait_ge(idx_made, (i + passes_before) * (RING // GRP) + q + 1)
                    gp.sem_inc(pool_step, 1)
                    for k in range(q * GRP, (q + 1) * GRP):
                        gp.indirect_dma_start(G[k][:, :], None, table,
                                              bass.IndirectOffsetOnAxis(ap=IDX[:, k:k + 1], axis=0))\
                            .then_inc(gath[k], 16)

            gp.sem_inc(ring_free, RING)
            gp.wait_ge(rec_in, 16)
            gp.wait_ge(xr_out, 16 * NREL * NT)
            with gp.Fori(0, PASSES) as i:
                gather(0, i, xr_d, 1)
            with gp.Fori(0, NL2) as l:
                gp.wait_ge(xg_out, (l + 1) * (16 * NT))
                gp.sem_inc(pool_step, 1)
                with gp.Fori(0, PASSES) as i:
                    for q in range(RING // GRP):
                        gp.wait_ge(ring_free, (l * PASSES + i + PASSES) * RING + GRP * (q + 1))
                        gp.sem_inc(pool_step, 1)
                        gp.tensor_copy(IDX[:, q * GRP:(q + 1) * GRP],
                                       RS[:, bass.ds(i * RING + q * GRP, GRP), 0]).then_inc(idx_made, 1)
                        gp.wait_ge(idx_made, (l * PASSES + i + PASSES) * (RING // GRP) + q + 1)
                        gp.sem_inc(pool_step, 1)
                        for k in range(q * GRP, (q + 1) * GRP):
                            gp.indirect_dma_start(G[k][:, :], None, xg_d,
                                                  bass.IndirectOffsetOnAxis(ap=IDX[:, k:k + 1], axis=0))\
                                .then_inc(gath[k], 16)

        @block.tensor
        def _(pe):
            def transposes(bank, rows, n=None):
                for k in range(KT):
                    mm = pe.transpose(ps[:, bank, k * P:(k + 1) * P], rows[:, k * P:(k + 1) * P], ident[:, :])
                mm.then_inc(tr_done, 1)

            def natural(bank, lt, w, n, first=True, last=True):
                for k in range(KT):
                    mm = pe.matmul(ps[:, bank, :], lt[:, k, n * P:(n + 1) * P], w[:, k, :],
                                   start=first and k == 0, stop=last and k == KT - 1)
                return mm

            def zeros(bank, open_):
                return pe.matmul(ps[:, bank, :], zero[:, 0:P], zero[:, :], start=open_, stop=not open_)

            pe.wait_ge(consts, 6)
            pe.wait_ge(x_in, 16 * NT)
            for n in range(NT):
                transposes(n, B[:, n, :])
            pe.wait_ge(tot_made, 1)
            tot = run[:, :, EC - 1]
            pe.matmul(ps[:, 7, 0:NT], tri[:, :], tot, start=True, stop=True)
            pe.matmul(ps[:, 7, NT:2 * NT], ones[:, :], tot, start=True, stop=True).then_inc(pre_made, 1)
            pe.wait_ge(tr_out, NT)
            for q in range(2 * NREL * NT):
                j, n = divmod(q, NT)
                slot_ = (0, 1, 2, 3, 0, 1)[j]
                if n == 0:
                    pe.wait_ge(w_in[slot_], 16 if j < 4 else 32)
                if q == 2:
                    pe.wait_ge(pre_read, 1)
                if q >= 8:
                    pe.wait_ge(prod_out, q - 7)
                natural((5 + q) % 8, XT, W[slot_], n).then_inc(prod_done, 1)
            pe.wait_ge(prod_out, 2 * NREL * NT)
            pe.wait_ge(bucket_made, 1)
            for b in range(7):
                zeros(b, True)
            with pe.Fori(0, PASSES) as i:
                for k in range(RING):
                    b = pe.value_load(tile_of[0:1, bass.ds(i * RING + k, 1)], min_val=0, max_val=NT - 1)
                    pe.wait_ge(oh_made, i * RING + k + 1)
                    pe.matmul(ps[:, b, :], SB[k % ZR][:, :], OS[k % ZR][:, 0:D],
                              start=False, stop=False, skip_group_check=True)
                    pe.matmul(ps_tail[:, bass.ds(b * P, P)], SB[k % ZR][:, :], OS[k % ZR][:, D:NP],
                              start=False, stop=False, skip_group_check=True).then_inc(oh_used, 1)
            for b in range(7):
                mm = zeros(b, False)
            mm.then_inc(cnt_done, 1)
            pe.wait_ge(cnt_out, 2 * NT)
            for a in range(NT):
                if a >= 3:
                    pe.wait_ge(adj_out, a - 2)
                for n in range(NT):
                    if a == 0:
                        pe.wait_ge(adj_made, n + 1)
                    o = ps[:, a, n * P:(n + 1) * P] if n < 4 else ps[:, 5 + a % 3, 0:P]
                    mm = pe.transpose(o, AN[:, n, a * P:(a + 1) * P], ident[:, :])
                mm.then_inc(adj_tr, 1)

            pe.wait_ge(adj_out, NT)
            for b in range(NT):
                zeros(b, True)
            with pe.Fori(0, PASSES) as i:
                for k in range(RING):
                    b = pe.value_load(tile_of[0:1, bass.ds(i * RING + k, 1)], min_val=0, max_val=NT - 1)
                    pe.wait_ge(gath[k], i * 16 + 16)
                    pe.wait_ge(s_made, i * RING + k + 1)
                    pe.matmul(ps[:, b, :], S[k % ZR][:, :], G[k][:, :],
                              start=False, stop=False, skip_group_check=True).then_inc(ring_free, 1)
            for b in range(NT):
                mm = zeros(b, False)
            mm.then_inc(acc_done, 1)

            def mean_layer(l, last_x, wcount):
                for n in range(NT):
                    pe.wait_ge(x_made, last_x + n + 1)
                    transposes((2 + n) % 5, X[:, n, :])
                for a in range(2 * KT):
                    f, hf = divmod(a, 2)
                    if a >= 3:
                        pe.wait_ge(tr_out, wcount["tr"] + a - 2)
                    for n in range(NT):
                        mm = pe.matmul(ps[:, (5, 6, 7, 2, 3, 4, 0, 1)[a], 0:HALF], X[:, n, f * P:(f + 1) * P],
                                       AT[:, n, hf * HALF:(hf + 1) * HALF], start=n == 0, stop=n == NT - 1)
                    mm.then_inc(agg_done, 1)
                pe.wait_ge(tr_out, wcount["tr"] + NT)
                for n in range(NT):
                    if n == 0:
                        pe.wait_ge(agg_out, wcount["agg"] + 3)
                        pe.wait_ge(w_in[3], wcount["w"])
                    if n == 3:
                        pe.wait_ge(agg_out, wcount["agg"] + 2 * KT)
                    natural((5, 6, 7, 0, 1)[n], XT, W[3], n, last=False)
                    if n == 0:
                        pe.wait_ge(agg_out, wcount["agg"] + 2 * KT)
                        pe.wait_ge(w_in[2], wcount["w"])
                    natural((5, 6, 7, 0, 1)[n], GT, W[2], n, first=False).then_inc(prod_done, 1)

            with pe.Fori(0, NL1) as l:
                mean_layer(l, l * NT, {"tr": l * NT + NT, "agg": l * (2 * KT), "w": l * 16 + 32})

            T2 = NT + NL1 * NT
            X2 = NT + NL1 * NT + NT
            with pe.Fori(0, NL2) as l:
                pe.wait_ge(x_made, l * NT + X2)
                for b in range(NT):
                    zeros(b, True)
                with pe.Fori(0, PASSES) as i:
                    for k in range(RING):
                        b = pe.value_load(tile_of[0:1, bass.ds(i * RING + k, 1)], min_val=0, max_val=NT - 1)
                        pe.wait_ge(s_made, (l * PASSES + i + PASSES) * RING + k + 1)
                        pe.wait_ge(z_made, (l * PASSES + i) * RING + k + 1)
                        pe.matmul(ps[:, b, :], S[k % ZR][:, :], Z[k % ZR][:, :],
                                  start=False, stop=False, skip_group_check=True).then_inc(z_free, 1)
                for b in range(NT):
                    mm = zeros(b, False)
                mm.then_inc(acc_done, 1)
                for n in range(NT):
                    pe.wait_ge(g_made, l * NT + n + 1)
                    if n >= 3:
                        pe.wait_ge(tr_out, l * NT + T2 + n - 2)
                    transposes(5 + n % 3, H[:, n, :])
                pe.wait_ge(tr_out, l * NT + T2 + NT)
                pe.wait_ge(w_in[0], l * 16 + 48)
                for a in range(2 * KT):
                    o, hf = divmod(a, 2)
                    for k in range(KT):
                        mm = pe.matmul(ps[:, (0, 1, 2, 3, 4, 7, 5, 6)[a], 0:HALF], W[0][:, k, o * P:(o + 1) * P],
                                       GT[:, k, hf * HALF:(hf + 1) * HALF], start=k == 0, stop=k == KT - 1)
                    mm.then_inc(ht_done, 1)
                pe.wait_ge(ht_out, l * KT + KT)
                pe.wait_ge(w_in[1], l * 16 + 48)
                for n in range(NT):
                    natural(n, HT, W[1], n).then_inc(prod_done, 1)

            mean_layer(NL1, X2 + NL2 * NT,
                       {"tr": T2 + NL2 * NT, "agg": NL1 * 2 * KT, "w": 16 * (NL1 + 2)})

        @block.scalar
        def _(act):
            def tr_evac(bank, to, n, count):
                act.wait_ge(tr_done, count)
                nc.scalar.copy(to[:, :, n * P:(n + 1) * P],
                               ps[:, bank, :].rearrange("p (k m) -> p k m", k=KT)).then_inc(tr_out, 1)

            def root(count, n):
                act.wait_ge(ln_var, count)
                nc.scalar.activation(sd[:, n:n + 1], mv[:, n, 1:2], ACT.Sqrt, bias=epst[:, 0:1])\
                    .then_inc(ln_sd, 1)

            for n in range(NT):
                tr_evac(n, XT, n, n + 1)
            act.wait_ge(cnt_done, 1)
            for b in range(NT):
                nc.scalar.activation(AN[:, b, 0:D], ps[:, b, :], ACT.Copy, accum_out=deg[:, 0, b:b + 1])\
                    .then_inc(cnt_out, 1)
                nc.scalar.activation(AN[:, b, D:NP], ps_tail[:, b * P:(b + 1) * P], ACT.Copy,
                                     accum_out=deg[:, 1, b:b + 1]).then_inc(cnt_out, 1)
            for a in range(NT):
                act.wait_ge(adj_tr, a + 1)
                nc.scalar.copy(AT[:, a, 0:D], ps[:, a, :])
                nc.scalar.copy(AT[:, a, D:NP], ps[:, 5 + a % 3, 0:P]).then_inc(adj_out, 1)

            def block_end(ln_before, x_before):
                for n in range(NT):
                    root(ln_before + n + 1, n)
                for n in range(NT):
                    act.wait_ge(x_made, x_before + n + 1)
                    nc.scalar.copy(B[:, n, :], X[:, n, :]).then_inc(b_made, 1)

            block_end(0, 0)

            def mean_layer(tr, agg, tr_base):
                for n in range(NT):
                    tr_evac((2 + n) % 5, XT, n, tr + n + 1)
                for a in range(2 * KT):
                    f, hf = divmod(a, 2)
                    act.wait_ge(agg_done, agg + a + 1)
                    nc.scalar.copy(GT[:, f, hf * HALF:(hf + 1) * HALF],
                                   ps[:, (5, 6, 7, 2, 3, 4, 0, 1)[a], 0:HALF]).then_inc(agg_out, 1)

            with act.Fori(0, NL1) as l:
                mean_layer(l * NT + NT, l * (2 * KT), None)
                for n in range(NT):
                    root(l * NT + NT + n + 1, n)
            block_end(NT + NL1 * NT, NT + NL1 * NT)

            X2 = NT + NL1 * NT + NT
            T2 = NT + NL1 * NT
            with act.Fori(0, NL2) as l:
                act.wait_ge(row_in[3], l * 16 + 32)
                act.wait_ge(x_made, l * NT + X2)
                nc.scalar.copy(we_psum, ROW[3][:, :]).then_inc(we_ok, 1)
                with act.Fori(0, PASSES) as i:
                    for k in range(RING):
                        act.wait_ge(ring_free, (l * PASSES + i + PASSES + 1) * RING + k + 1)
                        nc.scalar.activation(Z[k % ZR][:, :], Z[k % ZR][:, :], ACT.Relu).then_inc(z_made, 1)
                for n in range(NT):
                    tr_evac(5 + n % 3, GT, n, l * NT + T2 + n + 1)

                def norm(o):
                    act.wait_ge(bn_var, l * KT + o + 1)
                    nc.scalar.activation(sd[:, o:o + 1], mv[:, o, 1:2], ACT.Sqrt, bias=epst[:, 0:1])\
                        .then_inc(bn_sd, 1)
                    act.wait_ge(bn_sc, l * KT + o + 1)
                    nc.scalar.activation(HT[:, o, :], HT[:, o, :], ACT.Relu, bias=sc[:, 1, o:o + 1],
                                         scale=sc[:, 0, o:o + 1]).then_inc(ht_out, 1)

                act.wait_ge(lcol_made, l + 1)
                for a in range(2 * KT):
                    o, hf = divmod(a, 2)
                    act.wait_ge(ht_done, l * (2 * KT) + a + 1)
                    nc.scalar.activation(HT[:, o, hf * HALF:(hf + 1) * HALF],
                                         ps[:, (0, 1, 2, 3, 4, 7, 5, 6)[a], 0:HALF], ACT.Identity,
                                         bias=lcol[:, 0, o:o + 1]).then_inc(ht_raw, 1)
                    if hf == 1 and o >= 1:
                        norm(o - 1)
                norm(KT - 1)
            block_end(NT + NL1 * NT + NT, X2 + NL2 * NT)
            mean_layer(T2 + NL2 * NT, NL1 * 2 * KT, None)
            for n in range(NT):
                act.wait_ge(sg_in, n + 1)
                nc.scalar.activation(X[:, n, :], H[:, n, :], ACT.Sigmoid).then_inc(sg_out, 1)
            for n in range(NT):
                root(NT + NL1 * NT + NT + NT + n + 1, n)

        @block.vector
        def _(v):
            chain = Chain(v, dve)
            link = chain.link

            v.memset(B[:, NT - 1, :], 0.0).then_inc(tail_clear, 1)
            v.memset(PAD[:, :, :], 0)
            link(v.memset(one80[:, :], 0.0))
            v.memset(PAD[:, :, 2].bitcast(F32), -1.0).then_inc(pad_made, 1)
            v.memset(zero[:, :], 0.0)
            v.memset(epst[:, :], LN_EPS)

            v.wait_ge(edges_in, 64)
            link(v.tensor_scalar(ti[:, :], e_dst[:, :], 7, None, ALU.arith_shift_right))
            v.tensor_copy(bk[:, :], ti[:, :])
            link(v.tensor_scalar(ti2[:, :], e_dst[:, :], P - 1, None, ALU.bitwise_and))
            v.tensor_copy(REC[:, :, 2].bitcast(F32), ti2[:, :])
            v.tensor_copy(REC[:, :, 0], e_src[:, :])
            link(v.tensor_copy(REC[:, :, 3].bitcast(F32), e_w[:, :]))
            v.scalar_tensor_tensor(out=REC[:, :, 1], in0=e_typ[:, :], scalar=float(NP), in1=e_src[:, :],
                                   op0=ALU.mult, op1=ALU.add)
            for b in range(NT):
                ins = v.tensor_scalar(oh[:, b, :], bk[:, :], float(b), None, ALU.is_equal)
            link(ins)
            for b in range(NT):
                ins = v.tensor_tensor_scan(run[:, b, :], oh[:, b, :], one80[:, :], 0.0, ALU.add, ALU.add)
            ins.then_inc(tot_made, 1)
            v.wait_ge(pre_made, 1)
            link(v.tensor_scalar(basei[:, :], ps[:, 7, NT:2 * NT], float(P - 1), None, ALU.add))
            link(v.tensor_scalar(basei[:, :], basei[:, :], 7, None, ALU.arith_shift_right))
            link(v.tensor_copy(base[:, 0, :], basei[:, :]))
            link(v.memset(base[:, 3, :], 0.0))
            link(v.tensor_tensor_scan(base[:, 1, :], base[:, 0, :], base[:, 3, :], 0.0, ALU.add, ALU.add))
            link(v.tensor_tensor(base[:, 2, :], base[:, 1, :], base[:, 0, :], ALU.subtract))
            link(v.tensor_scalar(base[:, 2, :], base[:, 2, :], float(P), -1.0, ALU.mult, ALU.add))
            ins = v.tensor_tensor(base[:, 3, :], base[:, 2, :], ps[:, 7, 0:NT], ALU.add)
            link(ins)
            v.sem_inc(pre_read, 1)
            for b in range(NT):
                ins = v.scalar_tensor_tensor(out=run[:, b, :], in0=run[:, b, :], scalar=base[0:EP, 3, b:b + 1],
                                             in1=oh[:, b, :], op0=ALU.add, op1=ALU.mult)
            link(ins)
            link(v.tensor_reduce(slot[:, :], run[:, :, :].rearrange("p b c -> p c b"), AX_X, ALU.add))
            link(v.tensor_copy(ti[:, :], slot[:, :]))
            v.tensor_scalar(ti2[:, :], ti[:, :], P - 1, None, ALU.bitwise_and)
            link(v.tensor_scalar(ti[:, :], ti[:, :], 7, None, ALU.arith_shift_right))
            v.scalar_tensor_tensor(out=REC[:, :, 4], in0=ti2[:, :], scalar=float(TE), in1=ti[:, :],
                                   op0=ALU.mult, op1=ALU.add).then_inc(rec_made, 1)
            v.wait_ge(consts, 6)
            link(v.tensor_scalar(tf[:, 0, :], iota_t[:, :], base[0:1, 1, 0:1], None, ALU.is_ge))
            for b in range(1, NT - 1):
                link(v.scalar_tensor_tensor(out=tf[:, b % 2, :], in0=iota_t[:, :], scalar=base[0:1, 1, b:b + 1],
                                            in1=tf[:, 1 - b % 2, :], op0=ALU.is_ge, op1=ALU.add))
            v.tensor_copy(tile_of[:, :], tf[:, (NT - 2) % 2, :]).then_inc(bucket_made, 1)

            v.wait_ge(small_in, 48)
            for t in range(NREL):
                ins = v.tensor_scalar(mask[:, t, :], nti[:, :], float(t), None, ALU.is_equal)
            link(v.tensor_scalar(eps1[:, :], eps1[:, :], 1.0, None, ALU.add))
            for t in range(NREL):
                v.wait_ge(row_in[3 + t], 16)
            for q in range(NREL * NT):
                r, n = divmod(q, NT)
                v.wait_ge(prod_done, q + 1)
                v.wait_ge(row_in[r], 16)
                to = G[q][:, :] if q < RING else X[:, q - RING, :]
                v.tensor_tensor(to, ps[:, (5 + q) % 8, :], ROW[r][:, :], ALU.add).then_inc(prod_out, 1)
                if r == 0:
                    link(v.tensor_scalar(H[:, n, :], ROW[3][:, :], mask[:, 0, n:n + 1], None, ALU.mult))
                else:
                    link(v.scalar_tensor_tensor(out=H[:, n, :], in0=ROW[3 + r][:, :], scalar=mask[:, r, n:n + 1],
                                                in1=H[:, n, :], op0=ALU.mult, op1=ALU.add))
            for q in range(NREL * NT, 2 * NREL * NT):
                t, n = divmod(q - NREL * NT, NT)
                v.wait_ge(prod_done, q + 1)
                if t:
                    v.wait_ge(prod_out, q - NT + 1)
                v.scalar_tensor_tensor(out=H[:, n, :], in0=ps[:, (5 + q) % 8, :], scalar=mask[:, t, n:n + 1],
                                       in1=H[:, n, :], op0=ALU.mult, op1=ALU.add).then_inc(prod_out, 1)

            v.wait_ge(rec_in, 16)
            link(v.tensor_copy(srcf[:, :], RS[:, :, 0]))
            dl = RS[:, :, 2].bitcast(F32)
            wt = RS[:, :, 3].bitcast(F32)
            v.sem_inc(oh_used, ZR)
            with v.Fori(0, PASSES) as i:
                for k in range(RING):
                    v.wait_ge(oh_used, i * RING + k + 1)
                    v.tensor_scalar(SB[k % ZR][:, :], iota_h[:, 0:P], dl[:, bass.ds(i * RING + k, 1)], None,
                                    ALU.is_equal)
                    v.tensor_scalar(OS[k % ZR][:, :], iota_h[:, :], srcf[:, bass.ds(i * RING + k, 1)], None,
                                    ALU.is_equal).then_inc(oh_made, 1)
            for n in range(NT):
                v.wait_ge(cnt_out, 2 * n + 2)
                link(v.tensor_tensor(rstd[:, n:n + 1], deg[:, 0, n:n + 1], deg[:, 1, n:n + 1], ALU.add))
                link(v.tensor_scalar(rstd[:, n:n + 1], rstd[:, n:n + 1], 1.0, None, ALU.max))
                link(v.reciprocal(rstd[:, n:n + 1], rstd[:, n:n + 1]))
                v.tensor_scalar(AN[:, n, :], AN[:, n, :], rstd[:, n:n + 1], None, ALU.mult).then_inc(adj_made, 1)

            v.sem_inc(z_free, ZR)
            with v.Fori(0, PASSES) as i:
                for k in range(RING):
                    v.wait_ge(ring_free, i * RING + k + 1 + RING - ZR)
                    v.tensor_scalar(S[k % ZR][:, :], iota_f[:, :], dl[:, bass.ds(i * RING + k, 1)], None,
                                    ALU.is_equal).then_inc(s_made, 1)

            def stats(rows, n):
                link(v.bn_stats(st[:, n, 0, :], rows))
                v.sem_inc(dve_step, 1)
                v.bn_aggr(mv[:, n, :], st[:, n, 0, :]).then_inc(ln_var, 1)

            def normed(to, rows, n, ln_count):
                v.wait_ge(ln_sd, ln_count)
                link(v.reciprocal(rstd[:, n:n + 1], sd[:, n:n + 1]))
                return v.tensor_scalar(to, rows, mv[:, n, 0:1], rstd[:, n:n + 1], ALU.subtract, ALU.mult)

            v.wait_ge(acc_done, 1)
            for n in range(NT):
                link(v.tensor_tensor(H[:, n, :], ps[:, n, :], H[:, n, :], ALU.add))
                link(v.scalar_tensor_tensor(out=H[:, n, :], in0=H[:, n, :], scalar=0.0, in1=B[:, n, :],
                                            op0=ALU.max, op1=ALU.add))
                stats(H[:, n, :], n)
            for n in range(NT):
                normed(X[:, n, :], H[:, n, :], n, n + 1).then_inc(x_made, 1)

            def block_end(ln_before):
                for n in range(NT):
                    link(v.tensor_tensor(H[:, n, :], X[:, n, :], B[:, n, :], ALU.add))
                    stats(H[:, n, :], n)
                for n in range(NT):
                    normed(X[:, n, :], H[:, n, :], n, ln_before + n + 1).then_inc(x_made, 1)

            v.wait_ge(b_made, NT)
            PER1 = 6 * NT
            with v.Fori(0, NL1) as l:
                chain.enter(l * PER1)
                for n in range(NT):
                    v.wait_ge(prod_done, l * NT + 2 * NREL * NT + n + 1)
                    if n == 0:
                        for i in range(3):
                            v.wait_ge(row_in[i], l * 16 + 32)
                    link(v.tensor_tensor(H[:, n, :], ps[:, (5, 6, 7, 0, 1)[n], :], ROW[0][:, :], ALU.add))
                    stats(H[:, n, :], n)
                    link(normed(H[:, n, :], H[:, n, :], n, l * NT + NT + n + 1))
                    link(v.tensor_tensor(H[:, n, :], H[:, n, :], ROW[1][:, :], ALU.mult))
                    link(v.tensor_tensor(H[:, n, :], H[:, n, :], ROW[2][:, :], ALU.add))
                    ins = v.scalar_tensor_tensor(out=X[:, n, :], in0=H[:, n, :], scalar=0.0, in1=X[:, n, :],
                                                 op0=ALU.max, op1=ALU.add)
                    ins.then_inc(x_made, 1)
                chain.leave(PER1, NL1)
            block_end(NT + NL1 * NT)

            v.wait_ge(row_in[4], 32)
            X2 = NT + NL1 * NT + NT
            for n in range(NT):
                v.wait_ge(x_made, X2 - NT + n + 1)
                v.tensor_tensor(H[:, n, :], X[:, n, :], ROW[4][:, :], ALU.add).then_inc(xp_made, 1)
            v.wait_ge(b_made, 2 * NT)
            PER2 = 5 * KT + NT
            with v.Fori(0, NL2) as l:
                chain.enter(l * PER2)
                v.tensor_copy(lcol[:, :, :], colt[:, :, bass.ds(l, 1), :].rearrange("p a o k -> p a (o k)"))\
                    .then_inc(lcol_made, 1)
                v.wait_ge(we_ok, l + 1)
                v.sem_inc(dve_step, 1)
                with v.Fori(0, PASSES) as i:
                    for k in range(RING):
                        v.wait_ge(z_free, (l * PASSES + i) * RING + k + 1)
                        v.tensor_scalar(S[k % ZR][:, :], iota_f[:, :], dl[:, bass.ds(i * RING + k, 1)], None,
                                        ALU.is_equal).then_inc(s_made, 1)
                        v.wait_ge(gath[k], (l * PASSES + i + PASSES) * 16 + 16)
                        v.scalar_tensor_tensor(out=Z[k % ZR][:, :], in0=we_psum,
                                               scalar=wt[:, bass.ds(i * RING + k, 1)], in1=G[k][:, :],
                                               op0=ALU.mult, op1=ALU.add).then_inc(ring_free, 1)
                v.wait_ge(acc_done, l + 2)
                for n in range(NT):
                    v.scalar_tensor_tensor(out=H[:, n, :], in0=X[:, n, :], scalar=eps1[:, bass.ds(l, 1)],
                                           in1=ps[:, n, :], op0=ALU.mult, op1=ALU.add).then_inc(g_made, 1)
                for o in range(KT):
                    v.wait_ge(ht_raw, l * (2 * KT) + 2 * o + 1)
                    link(v.bn_stats(st[:, o, 0, :], HT[:, o, 0:HALF]))
                    v.wait_ge(ht_raw, l * (2 * KT) + 2 * o + 2)
                    link(v.bn_stats(st[:, o, 1, :], HT[:, o, HALF:N]))
                    v.sem_inc(dve_step, 1)
                    ins = v.bn_aggr(mv[:, o, :], st[:, o, :, :].rearrange("p a s -> p (a s)"))
                    ins.then_inc(bn_var, 1)
                    v.wait_ge(bn_sd, l * KT + o + 1)
                    link(v.reciprocal(rstd[:, o:o + 1], sd[:, o:o + 1]))
                    link(v.tensor_tensor(sc[:, 0, o:o + 1], rstd[:, o:o + 1], lcol[:, 1, o:o + 1],
                                         ALU.mult))
                    link(v.tensor_tensor(msc[:, o:o + 1], mv[:, o, 0:1], sc[:, 0, o:o + 1], ALU.mult))
                    v.tensor_tensor(sc[:, 1, o:o + 1], lcol[:, 2, o:o + 1], msc[:, o:o + 1],
                                    ALU.subtract).then_inc(bn_sc, 1)
                v.wait_ge(row_in[5], l * 16 + 32)
                v.wait_ge(row_in[4], l * 16 + 48)
                for n in range(NT):
                    v.wait_ge(prod_done, l * NT + (2 * NREL + NL1) * NT + n + 1)
                    link(v.tensor_tensor(X[:, n, :], ps[:, n, :], ROW[5][:, :], ALU.add))
                    v.scalar_tensor_tensor(out=H[:, n, :], in0=X[:, n, :], scalar=0.0, in1=ROW[4][:, :],
                                           op0=ALU.max, op1=ALU.add).then_inc(xp_made, 1)
                    v.tensor_scalar(X[:, n, :], X[:, n, :], 0.0, None, ALU.max).then_inc(x_made, 1)
                chain.leave(PER2, NL2)
            v.wait_ge(x_made, X2 + NL2 * NT)
            block_end(NT + NL1 * NT + NT)

            v.wait_ge(row_in[0], 16 * (NL1 + 2))
            v.wait_ge(b_made, 3 * NT)
            PR3 = (2 * NREL + NL1 + NL2) * NT
            for n in range(NT):
                v.wait_ge(prod_done, PR3 + n + 1)
                v.tensor_tensor(H[:, n, :], ps[:, (5, 6, 7, 0, 1)[n], :], ROW[0][:, :], ALU.add).then_inc(sg_in, 1)
                v.wait_ge(sg_out, n + 1)
                link(v.tensor_tensor(X[:, n, :], X[:, n, :], H[:, n, :], ALU.mult))
                link(v.tensor_tensor(X[:, n, :], X[:, n, :], B[:, n, :], ALU.add))
                stats(X[:, n, :], n)
            for n in range(NT):
                normed(H[:, n, :], X[:, n, :], n, NT + NL1 * NT + NT + NT + n + 1).then_inc(o_made, 1)


def kernel(**inputs):
    import concourse.bacc as _bacc
    from concourse.bass_utils import run_bass_kernel_spmd as _run

    a = {k: np.asarray(v) for k, v in inputs.items()}
    nodes = np.pad(a["node_type_3"], (0, NP - N)).reshape(NT, P).T
    cols = np.stack([a["L2_gnn_" + c].reshape(NL2, KT, P).transpose(2, 0, 1) for c in ("b1", "gamma", "beta")],
                    axis=1)
    again = lambda r: np.concatenate([r, r[:1]])
    given = {
        "x": a["x"], "src": a["src"].reshape(EP, EC), "dst": a["dst"].reshape(EP, EC),
        "etype": a["edge_type_3"].reshape(EP, EC), "ew": a["edge_weight1"].reshape(EP, EC), "ntype": nodes,
        "w_rel": a["L0_gnn_W_rel"], "b_rel": a["L0_gnn_b_rel"],
        "w_self": a["L0_gnn_W_self"], "b_self": a["L0_gnn_b_self"],
        "wlt": a["L1_gnn_W_l"].transpose(0, 2, 1), "wrt": a["L1_gnn_W_r"].transpose(0, 2, 1),
        "b1_l1": a["L1_gnn_b"], "ln_g": a["L1_gnn_ln_g"], "ln_b": a["L1_gnn_ln_b"],
        "eps": a["L2_gnn_eps"].reshape(1, NL2), "we": again(a["L2_gnn_We"].reshape(NL2, D)),
        "be": again(a["L2_gnn_be"]), "w1": a["L2_gnn_W1"], "w2": a["L2_gnn_W2"], "cols": cols,
        "b2": a["L2_gnn_b2"], "w3l": a["L3_gnn_W_l"], "w3r": a["L3_gnn_W_r"], "b3": a["L3_gnn_b"].reshape(1, D),
    }
    nc = _bacc.Bacc("TRN2", target_bir_lowering=False, num_devices=1)
    arrays, args = {}, []
    for name, v in given.items():
        arrays[f"in_{name}"] = np.ascontiguousarray(v)
        args.append(nc.dram_tensor(f"in_{name}", v.shape, mybir.dt.from_np(v.dtype), kind="ExternalInput").ap())
    args.append(nc.dram_tensor("out_0", (N, D), F32, kind="ExternalOutput").ap())
    build(nc, *args)
    return _run(nc, [arrays], core_ids=[0]).results[0]["out_0"]
```

```python
from contextlib import ExitStack

import numpy as np

import concourse.bass as bass
from concourse import mybir

ALU = mybir.AluOpType
ACT = mybir.ActivationFunctionType
AX_X = mybir.AxisListType.X
F32 = mybir.dt.float32
F16 = mybir.dt.float16
BF16 = mybir.dt.bfloat16
F32R = mybir.dt.float32r
I32 = mybir.dt.int32

P = 128
N = 625
D = 512
E = 10000
NT = -(-N // P)
NP = NT * P
LAST = N - (NT - 1) * P
KT = D // P
HALF = NP // 2
EP = 125
EC = E // EP
RING = 12
GRP = 4
TE = -(-((E - NT) // P + NT) // RING) * RING
PASSES = TE // RING
PACK = 6
BITS = 3
BASE = 1 << BITS
OR = 6
ZR = 4
RECW = 5
HJOBS = ((0, 0), (1, 0), (0, 1), (1, 1), (2, 0), (2, 1), (3, 0), (3, 1))
HBANKS = (0, 1, 2, 3, 4, 7, 5, 6)
HI, LO = 0, 1
THREE = ((HI, HI), (HI, LO), (LO, HI))
LN_EPS = 1e-5
NREL = 3
NL1 = 3
NL2 = 4


class Chain:

    def __init__(self, eng, sem):
        self.eng, self.sem, self.n, self.reg = eng, sem, 0, None

    def link(self, ins):
        self.n += 1
        ins.then_inc(self.sem, 1)
        self.eng.wait_ge(self.sem, self.n if self.reg is None else self.reg + self.n)

    def enter(self, reg_part):
        self.reg, self.start = reg_part, self.n

    def leave(self, per, times):
        assert self.n - self.start == per, (self.n - self.start, per)
        self.reg = None
        self.n = self.start + per * times


def build(nc, x, src, dst, etype, ew, ntype, weights, b_rel, b_self, b1_l1, ln_g, ln_b,
          eps, we, be, cols, b2, b3, out):
    rec_d = nc.dram_tensor("edge_records", (P * TE, 4), I32).ap()
    xr_d = nc.dram_tensor("rel_rows", (NREL * NP, D), F32).ap()
    xg_d = nc.dram_tensor("gine_rows", (NP, D), F32).ap()

    with ExitStack() as ctx:
        def sb(name, shape, dt=F32):
            return ctx.enter_context(nc.sbuf_tensor(name, shape, dt))

        def sem(name):
            return ctx.enter_context(nc.semaphore(name))

        B = sb("block_in", [P, NT, D])
        X = sb("x_cur", [P, NT, D])
        H = sb("work", [P, NT, D])
        XT = sb("xT", [P, 2, KT, NP], F32R)
        GT = sb("gT", [P, 2, KT, NP], F32R)
        HR = H[:, :, :].rearrange("p t d -> p (t d)").rearrange("p (k n) -> p k n", k=KT)
        AT = sb("adjT", [P, 2, NT, NP], F32R)
        AN = X
        AN_tail = sb("adj_tail", [P, NT, P])
        W = [sb(f"w{i}", [P, 2, KT, D], F32R) for i in range(2)]
        ROW = [sb(f"row{i}", [P, D]) for i in range(6)]
        Z = sb("edge_rows", [P, ZR, D])
        assert ZR == KT
        WS = [sb("w_stage", [P, KT, D]), Z]
        S = [sb(f"onehot_dst{i}", [P, P]) for i in range(ZR)]
        SB = [sb(f"onehot_dst_b{i}", [P, P], BF16) for i in range(OR)]
        OS = [sb(f"onehot_src{i}", [P, NP], BF16) for i in range(OR)]
        RS = sb("records", [P, TE, 4], I32)
        srcf = sb("srcf", [P, TE])
        packed = sb("buckets_packed", [1, TE // PACK], I32)
        e_dst = sb("e_dst", [EP, EC], I32)
        e_src = sb("e_src", [EP, EC], I32)
        e_typ = sb("e_typ", [EP, EC], I32)
        e_w = sb("e_w", [EP, EC])
        REC = sb("rec_sb", [EP, EC, RECW], I32)
        PAD = RS
        ti = sb("ti", [EP, EC], I32)
        ti2 = sb("ti2", [EP, EC], I32)
        bk = sb("bk", [EP, EC])
        oh = sb("oh", [EP, NT, EC])
        run = sb("run", [EP, NT, EC])
        one80 = sb("one80", [EP, EC])
        slot = sb("slot", [EP, EC])
        tri = sb("tri", [EP, P])
        ones = sb("ones", [EP, P])
        base = sb("base", [P, 4, NT])
        basei = sb("basei", [P, NT], I32)
        tf = H[0:1, :, :].rearrange("o t d -> o (t d)")[:, 0:2 * TE].rearrange("o (a t) -> o a t", a=2)
        iota_f = sb("iota_f", [P, P])
        iota_h = sb("iota_h", [P, NP], F16)
        iota_t = sb("iota_t", [1, TE])
        ident = sb("ident", [P, P])
        zero = sb("zero", [P, D], BF16)
        epst = sb("epst", [P, 1])
        nti = sb("nti", [P, NT], I32)
        mask = sb("mask", [P, NREL, NT])
        eps1 = sb("eps1", [P, NL2])
        colt = sb("colt", [P, 3, NL2, KT])
        lcol = sb("lcol", [P, 3, KT])
        st = sb("st", [P, NT, 2, 6])
        msc = sb("msc", [P, KT])
        mv = sb("mv", [P, NT, 2])
        sd = sb("sd", [P, NT])
        rstd = sb("rstd", [P, NT])
        deg = sb("deg", [P, 2, NT])
        sc = sb("sc", [P, 2, KT])
        with ExitStack() as ring:
            G = [ring.enter_context(nc.sbuf_tensor(f"gathered{i}", [P, D], F32)) for i in range(RING)]
        XS = sb("x_parts", [P, 2, NT, D], F32R)
        ps = ctx.enter_context(nc.psum_tensor("ps", [P, 8, D], F32))
        ps_tail = ps[:, 5:7, :].rearrange("p a n -> p (a n)")

        consts = sem("consts")
        tri0 = sem("tri0")
        edges_in = sem("edges_in")
        small_in = sem("small_in")
        x_in = sem("x_in")
        tail_clear = sem("tail_clear")
        pad_made = sem("pad_made")
        pad_out = sem("pad_out")
        ws_in = [sem(f"w_stage{i}_in") for i in range(2)]
        w_hi = sem("w_hi")
        w_split = sem("w_split")
        xs_hi = sem("xs_hi")
        xs_made = sem("xs_made")
        row_in = [sem(f"row{i}_in") for i in range(6)]
        dve = sem("dve_chain")
        dve_step = sem("dve_step")
        lcol_made = sem("lcol_made")
        tot_made = sem("tot_made")
        pre_made = sem("pre_made")
        pre_read = sem("pre_read")
        rec_made = sem("rec_made")
        scat = sem("scattered")
        sp_step = sem("sp_step")
        pool_step = sem("pool_step")
        rec_in = sem("rec_in")
        rec_ok = sem("rec_ok")
        bucket_made = sem("bucket_made")
        oh_made = sem("onehots_made")
        oh_used = sem("onehots_used")
        cnt_done = sem("counts_done")
        cnt_out = sem("counts_out")
        adj_made = sem("adj_made")
        adj_tr = sem("adj_tr")
        adj_hi = sem("adj_hi")
        adj_out = sem("adj_out")
        tr_done = sem("tr_done")
        tr_hi = sem("tr_hi")
        tr_out = sem("tr_out")
        prod_done = sem("prod_done")
        prod_out = sem("prod_out")
        xr_out = sem("xr_out")
        ring_free = sem("ring_free")
        gath = [sem(f"gath{i}") for i in range(RING)]
        s_made = sem("onehot_made")
        z_free = sem("z_free")
        z_made = sem("z_relu")
        acc_open = sem("acc_open")
        acc_done = sem("acc_done")
        x_made = sem("x_made")
        b_made = sem("b_made")
        ln_var = sem("ln_var")
        ln_sd = sem("ln_sd")
        agg_done = sem("agg_done")
        agg_hi = sem("agg_hi")
        agg_out = sem("agg_out")
        we_ok = sem("we_ok")
        xp_made = sem("xp_made")
        xg_out = sem("xg_out")
        g_made = sem("g_made")
        ht_done = sem("ht_done")
        ht_raw = sem("ht_raw")
        bn_var = sem("bn_var")
        bn_sd = sem("bn_sd")
        ht_norm = sem("ht_norm")
        ht_hi = sem("ht_hi")
        ht_out = sem("ht_out")
        sg_in = sem("sg_in")
        sg_out = sem("sg_out")
        o_made = sem("o_made")
        o_out = sem("o_out")
        we_psum = ps[:, 5, :]

        xv = [x[n * P:min(N, n * P + P), :] for n in range(NT)]
        block = ctx.enter_context(nc.Block())

        @block.sync
        def _(sp):
            def w_load(j):
                sp.dma_start(WS[j % 2][:, :, :], weights[j].rearrange("(k p) n -> p k n", p=P))\
                    .then_inc(ws_in[j % 2], 16)

            def w_load_of(l, j):
                sp.dma_start(WS[j % 2][:, :, :],
                             weights[bass.ds(2 * l + j, 1), :, :].rearrange("o (k p) n -> p (o k) n", p=P))\
                    .then_inc(ws_in[j % 2], 16)

            def row_load(i, r):
                sp.dma_start(ROW[i][:, :], r.broadcast_to([P, D])).then_inc(row_in[i], 16)

            for t, d in ((e_dst, dst), (e_src, src), (e_typ, etype), (e_w, ew)):
                sp.dma_start(t[:, :], d).then_inc(edges_in, 16)
            for n in range(NT - 1):
                sp.dma_start(B[:, n, :], xv[n]).then_inc(x_in, 16)
            sp.wait_ge(tail_clear, 1)
            sp.dma_start(B[0:LAST, NT - 1, :], xv[NT - 1]).then_inc(x_in, 16)
            w_load(0)
            w_load(1)
            sp.dma_start(nti[:, :], ntype).then_inc(small_in, 16)
            sp.dma_start(eps1[:, :], eps.broadcast_to([P, NL2])).then_inc(small_in, 16)
            sp.dma_start(colt[:, :, :, :], cols).then_inc(small_in, 16)
            sp.wait_ge(pad_made, 1)
            sp.dma_start(rec_d.rearrange("(p t) r -> p t r", p=P), PAD[:, :, :]).then_inc(pad_out, 16)
            for r in range(NREL):
                row_load(r, b_rel[r:r + 1, :])
                row_load(3 + r, b_self[r:r + 1, :])
            for j in (2, 3):
                sp.wait_ge(w_split, j - 1)
                w_load(j)
            for q in range(NREL * NT):
                sp.wait_ge(prod_out, q + 1)
                r, n = divmod(q, NT)
                rows = G[q] if q < RING else X[:, q - RING]
                sp.dma_start(xr_d[r * NP + n * P:r * NP + (n + 1) * P, :], rows[:, :] if q < RING else rows)\
                    .then_inc(xr_out, 16)
            for j in (4, 5):
                sp.wait_ge(w_split, j - 1)
                w_load(j)
            sp.wait_ge(scat, 16 * EC)
            sp.dma_start(RS[:, :, :], rec_d.rearrange("(p t) r -> p t r", p=P)).then_inc(rec_in, 16)

            for j in (6, 7):
                sp.wait_ge(w_split, j - 1)
                w_load(j)
            with sp.Fori(0, NL1) as l:
                sp.wait_ge(x_made, l * NT + NT)
                sp.sem_inc(sp_step, 1)
                for i, r in ((0, b1_l1), (1, ln_g), (2, ln_b)):
                    sp.dma_start(ROW[i][:, :], r[bass.ds(l, 1), :].broadcast_to([P, D])).then_inc(row_in[i], 16)
                for j in (0, 1):
                    sp.wait_ge(w_split, 2 * l + 7 + j)
                    sp.sem_inc(sp_step, 1)
                    w_load_of(l, 8 + j)
            row_load(3, we[0:1, :])
            row_load(4, be[0:1, :])
            with sp.Fori(0, NL2) as l:
                for n in range(NT):
                    sp.wait_ge(xp_made, l * NT + n + 1)
                    sp.dma_start(xg_d[n * P:(n + 1) * P, :], H[:, n, :]).then_inc(xg_out, 16)
                sp.dma_start(ROW[5][:, :], b2[bass.ds(l, 1), :].broadcast_to([P, D])).then_inc(row_in[5], 16)
                sp.dma_start(ROW[4][:, :], be[bass.ds(l + 1, 1), :].broadcast_to([P, D])).then_inc(row_in[4], 16)
                sp.wait_ge(we_ok, l + 1)
                sp.sem_inc(sp_step, 1)
                sp.dma_start(ROW[3][:, :], we[bass.ds(l + 1, 1), :].broadcast_to([P, D])).then_inc(row_in[3], 16)
                sp.wait_ge(w_split, 2 * l + 13)
                sp.sem_inc(sp_step, 1)
                w_load_of(l, 14)
                sp.wait_ge(acc_done, l * NT + 2 * NT)
                sp.sem_inc(sp_step, 1)
                w_load_of(l, 15)
            row_load(0, b3)
            for n in range(NT):
                sp.wait_ge(o_made, n + 1)
                rows = P if n < NT - 1 else LAST
                sp.dma_start(out[n * P:n * P + rows, :], H[0:rows, n, :]).then_inc(o_out, 16)
            sp.wait_ge(o_out, 16 * NT)
            sp.wait_ge(row_in[3], 16 * (NL2 + 2))
            sp.wait_ge(row_in[4], 16 * (NL2 + 2))

        @block.gpsimd
        def _(gp):
            gp.memset(tri[:, :], 1.0).then_inc(tri0, 1)
            gp.memset(ident[:, :], 0.0).then_inc(tri0, 1)
            gp.memset(ones[:, :], 1.0).then_inc(consts, 1)
            gp.wait_ge(tri0, 2)
            gp.affine_select(out=tri[:, :], in_=tri[:, :], compare_op=ALU.is_gt, fill=0.0, base=0,
                             pattern=[[1, P]], channel_multiplier=-1).then_inc(consts, 1)
            gp.affine_select(out=ident[:, :], in_=ident[:, :], compare_op=ALU.not_equal, fill=1.0, base=0,
                             pattern=[[-1, P]], channel_multiplier=1).then_inc(consts, 1)
            gp.iota(iota_f[:, :], [[1, P]], base=0, channel_multiplier=0,
                    allow_small_or_imprecise_dtypes=True).then_inc(consts, 1)
            gp.iota(iota_h[:, :], [[1, NP]], base=0, channel_multiplier=0,
                    allow_small_or_imprecise_dtypes=True).then_inc(consts, 1)
            gp.iota(iota_t[:, :], [[1, TE]], base=0, channel_multiplier=0,
                    allow_small_or_imprecise_dtypes=True).then_inc(consts, 1)

            gp.wait_ge(pad_out, 16)
            gp.wait_ge(rec_made, 1)
            for c in range(EC):
                gp.indirect_dma_start(rec_d, bass.IndirectOffsetOnAxis(ap=REC[:, c, 4:5], axis=0),
                                      REC[:, c, 0:4], None).then_inc(scat, 16)

            def gather(table, column, used):
                for t in range(TE):
                    if t % GRP == 0:
                        gp.wait_ge(ring_free, used + t + GRP)
                        gp.sem_inc(pool_step, 1)
                    gp.indirect_dma_start(G[t % RING][:, :], None, table,
                                          bass.IndirectOffsetOnAxis(ap=RS[:, t, column:column + 1], axis=0))\
                        .then_inc(gath[t % RING], 16)

            gp.sem_inc(ring_free, RING)
            gp.wait_ge(rec_in, 16)
            gp.wait_ge(xr_out, 16 * NREL * NT)
            gather(xr_d, 1, 0)
            with gp.Fori(0, NL2) as l:
                gp.wait_ge(xg_out, (l + 1) * (16 * NT))
                gp.sem_inc(pool_step, 1)
                gather(xg_d, 0, l * TE + TE)

        @block.tensor
        def _(pe):
            def transposes(bank, rows, n=None):
                for k in range(KT):
                    mm = pe.transpose(ps[:, bank, k * P:(k + 1) * P], rows[:, k * P:(k + 1) * P], ident[:, :])
                mm.then_inc(tr_done, 1)

            def natural(bank, lt, w, n, first=True, last=True):
                for k in range(KT):
                    for a, b in THREE:
                        mm = pe.matmul(ps[:, bank, :], lt[:, a, k, n * P:(n + 1) * P], w[:, b, k, :],
                                       start=first and k == 0 and (a, b) == THREE[0],
                                       stop=last and k == KT - 1 and (a, b) == THREE[-1])
                return mm

            def zeros(bank, open_):
                return pe.matmul(ps[:, bank, :], zero[:, 0:P], zero[:, :], start=open_, stop=not open_)

            def buckets(i, k):
                word = pe.value_load(packed[0:1, bass.ds(i * (RING // PACK) + k // PACK, 1)],
                                     min_val=0, max_val=BASE ** PACK - 1)
                return [pe.snap((word >> (BITS * m)) & (BASE - 1), min_val=0, max_val=NT - 1) for m in range(PACK)]

            pe.wait_ge(consts, 6)
            pe.wait_ge(tot_made, 1)
            tot = run[:, :, EC - 1]
            pe.matmul(ps[:, 7, 0:NT], tri[:, :], tot, start=True, stop=True)
            pe.matmul(ps[:, 7, NT:2 * NT], ones[:, :], tot, start=True, stop=True).then_inc(pre_made, 1)
            pe.wait_ge(x_in, 16 * NT)
            for n in range(NT):
                transposes(n, B[:, n, :])
            pe.wait_ge(tr_out, NT)
            for q in range(2 * NREL * NT):
                j, n = divmod(q, NT)
                if n == 0:
                    pe.wait_ge(w_split, j + 1)
                if q == 2:
                    pe.wait_ge(pre_read, 1)
                if q >= 8:
                    pe.wait_ge(prod_out, q - 7)
                natural((5 + q) % 8, XT, W[j % 2], n).then_inc(prod_done, 1)
            pe.wait_ge(prod_out, 2 * NREL * NT)
            pe.wait_ge(bucket_made, 1)
            for b in range(7):
                zeros(b, True)
            with pe.Fori(0, PASSES) as i:
                for k in range(RING):
                    if k % PACK == 0:
                        banks = buckets(i, k)
                    b = banks[k % PACK]
                    if k % (OR // 2) == 0:
                        pe.wait_ge(oh_made, i * RING + k + OR // 2)
                    pe.matmul(ps[:, b, :], SB[k % OR][:, :], OS[k % OR][:, 0:D],
                              start=False, stop=False, skip_group_check=True)
                    pe.matmul(ps_tail[:, bass.ds(b * P, P)], SB[k % OR][:, :], OS[k % OR][:, D:NP],
                              start=False, stop=False, skip_group_check=True).then_inc(oh_used, 1)
            for b in range(7):
                mm = zeros(b, False)
            mm.then_inc(cnt_done, 1)
            pe.wait_ge(cnt_out, 2 * NT)
            for a in range(NT):
                if a >= 3:
                    pe.wait_ge(adj_out, a - 2)
                for n in range(NT):
                    if a == 0:
                        pe.wait_ge(adj_made, n + 1)
                    o = ps[:, a, n * P:(n + 1) * P] if n < 4 else ps[:, 5 + a % 3, 0:P]
                    i = AN[:, n, a * P:(a + 1) * P] if a < KT else AN_tail[:, n, :]
                    mm = pe.transpose(o, i, ident[:, :])
                mm.then_inc(adj_tr, 1)

            pe.wait_ge(adj_out, NT)
            for b in range(NT):
                zeros(b, True)
            with pe.Fori(0, PASSES) as i:
                for k in range(RING):
                    if k % PACK == 0:
                        banks = buckets(i, k)
                    b = banks[k % PACK]
                    if k % 2 == 0:
                        pe.wait_ge(gath[k], i * 16 + 16)
                        pe.wait_ge(gath[k + 1], i * 16 + 16)
                        pe.wait_ge(s_made, i * RING + k + 2)
                    pe.matmul(ps[:, b, :], S[k % ZR][:, :], G[k][:, :],
                              start=False, stop=False, skip_group_check=True).then_inc(ring_free, 1)
            for b in range(NT):
                zeros(b, False).then_inc(acc_done, 1)

            def mean_layer(l, last_x, wcount):
                for n in range(NT):
                    pe.wait_ge(x_made, last_x + n + 1)
                    transposes((2 + n) % 5, X[:, n, :])
                for a in range(2 * KT):
                    f, hf = divmod(a, 2)
                    if a >= 3:
                        pe.wait_ge(tr_out, wcount["tr"] + a - 2)
                    for n in range(NT):
                        if a == 0:
                            pe.wait_ge(xs_made, wcount["xs"] + n + 1)
                        for p, q in THREE:
                            mm = pe.matmul(ps[:, (5, 6, 7, 2, 3, 4, 0, 1)[a], 0:HALF],
                                           XS[:, p, n, f * P:(f + 1) * P],
                                           AT[:, q, n, hf * HALF:(hf + 1) * HALF],
                                           start=n == 0 and (p, q) == THREE[0],
                                           stop=n == NT - 1 and (p, q) == THREE[-1])
                    mm.then_inc(agg_done, 1)
                pe.wait_ge(tr_out, wcount["tr"] + NT)
                for n in range(NT):
                    if n == 0:
                        pe.wait_ge(agg_out, wcount["agg"] + 3)
                        pe.wait_ge(w_split, wcount["w"] + 1)
                    if n == 3:
                        pe.wait_ge(agg_out, wcount["agg"] + 2 * KT)
                    natural((5, 6, 7, 0, 1)[n], XT, W[0], n, last=False)
                    if n == 0:
                        pe.wait_ge(agg_out, wcount["agg"] + 2 * KT)
                        pe.wait_ge(w_split, wcount["w"] + 2)
                    natural((5, 6, 7, 0, 1)[n], GT, W[1], n, first=False).then_inc(prod_done, 1)

            with pe.Fori(0, NL1) as l:
                mean_layer(l, l * NT, {"tr": l * NT + NT, "agg": l * (2 * KT), "w": l * 2 + 6, "xs": l * NT})

            T2 = NT + NL1 * NT
            X2 = NT + NL1 * NT + NT
            with pe.Fori(0, NL2) as l:
                pe.wait_ge(x_made, l * NT + X2)
                for b in range(NT):
                    zeros(b, True)
                with pe.Fori(0, PASSES) as i:
                    for k in range(RING):
                        if k % PACK == 0:
                            banks = buckets(i, k)
                        b = banks[k % PACK]
                        if k % 2 == 0:
                            pe.wait_ge(s_made, (l * PASSES + i + PASSES) * RING + k + 2)
                            pe.wait_ge(z_made, (l * PASSES + i) * RING + k + 2)
                        pe.matmul(ps[:, b, :], S[k % ZR][:, :], Z[:, k % ZR, :],
                                  start=False, stop=False, skip_group_check=True).then_inc(z_free, 1)
                for b in range(NT):
                    zeros(b, False).then_inc(acc_done, 1)
                for n in range(NT):
                    pe.wait_ge(g_made, l * NT + n + 1)
                    if n >= 3:
                        pe.wait_ge(tr_out, l * NT + T2 + n - 2)
                    transposes(5 + n % 3, H[:, n, :])
                pe.wait_ge(w_split, l * 2 + 13)
                for a, (o, hf) in enumerate(HJOBS):
                    if a == 0:
                        pe.wait_ge(tr_out, l * NT + T2 + 3)
                    if a == 2:
                        pe.wait_ge(tr_out, l * NT + T2 + NT)
                    for k in range(KT):
                        for p, q in THREE:
                            mm = pe.matmul(ps[:, HBANKS[a], 0:HALF],
                                           W[0][:, p, k, o * P:(o + 1) * P],
                                           GT[:, q, k, hf * HALF:(hf + 1) * HALF],
                                           start=k == 0 and (p, q) == THREE[0],
                                           stop=k == KT - 1 and (p, q) == THREE[-1])
                    mm.then_inc(ht_done, 1)
                pe.wait_ge(w_split, l * 2 + 14)
                pe.wait_ge(ht_raw, l * (2 * KT) + NT)
                for k in range(KT):
                    pe.wait_ge(ht_out, l * KT + k + 1)
                    for n in range(NT):
                        for p, q in THREE:
                            mm = pe.matmul(ps[:, n, :], XT[:, p, k, n * P:(n + 1) * P], W[1][:, q, k, :],
                                           start=k == 0 and (p, q) == THREE[0],
                                           stop=k == KT - 1 and (p, q) == THREE[-1])
                        if k == KT - 1:
                            mm.then_inc(prod_done, 1)

            mean_layer(NL1, X2 + NL2 * NT,
                       {"tr": T2 + NL2 * NT, "agg": NL1 * 2 * KT, "w": 20, "xs": NT + NL1 * NT})

        @block.scalar
        def _(act):
            def tr_evac(bank, to, n, count):
                act.wait_ge(tr_done, count)
                nc.scalar.copy(to[:, HI, :, n * P:(n + 1) * P],
                               ps[:, bank, :].rearrange("p (k m) -> p k m", k=KT)).then_inc(tr_hi, 1)

            def w_high(j, landed, done):
                act.wait_ge(ws_in[j % 2], landed)
                if done is not None:
                    act.wait_ge(prod_done, done)
                for k in range(KT):
                    ins = nc.scalar.copy(W[j % 2][:, HI, k, :], WS[j % 2][:, k, :])
                ins.then_inc(w_hi, 1)

            def x_high(n, count):
                act.wait_ge(x_made, count)
                nc.scalar.copy(XS[:, HI, n, :], X[:, n, :]).then_inc(xs_hi, 1)

            def root(count, n):
                act.wait_ge(ln_var, count)
                nc.scalar.activation(sd[:, n:n + 1], mv[:, n, 1:2], ACT.Sqrt, bias=epst[:, 0:1])\
                    .then_inc(ln_sd, 1)

            for n in range(NT):
                tr_evac(n, XT, n, n + 1)
            for j in range(2 * NREL):
                w_high(j, 16 * (j // 2 + 1), NT * (j - 1) if j >= 2 else None)
            act.wait_ge(cnt_done, 1)
            for b in range(NT):
                nc.scalar.activation(AN[:, b, 0:D], ps[:, b, :], ACT.Copy, accum_out=deg[:, 0, b:b + 1])\
                    .then_inc(cnt_out, 1)
                nc.scalar.activation(AN_tail[:, b, :], ps_tail[:, b * P:(b + 1) * P], ACT.Copy,
                                     accum_out=deg[:, 1, b:b + 1]).then_inc(cnt_out, 1)
            for a in range(NT):
                act.wait_ge(adj_tr, a + 1)
                nc.scalar.copy(AT[:, HI, a, 0:D], ps[:, a, :])
                nc.scalar.copy(AT[:, HI, a, D:NP], ps[:, 5 + a % 3, 0:P]).then_inc(adj_hi, 1)

            def block_end(ln_before, x_before, parts):
                for n in range(NT):
                    root(ln_before + n + 1, n)
                for n in range(NT):
                    if parts:
                        x_high(n, x_before + n + 1)
                    act.wait_ge(x_made, x_before + n + 1)
                    nc.scalar.copy(B[:, n, :], X[:, n, :]).then_inc(b_made, 1)

            block_end(0, 0, True)

            def mean_layer(tr, agg, landed, done):
                for n in range(NT):
                    tr_evac((2 + n) % 5, XT, n, tr + n + 1)
                w_high(0, landed, done)
                w_high(1, landed, None)
                for a in range(2 * KT):
                    f, hf = divmod(a, 2)
                    act.wait_ge(agg_done, agg + a + 1)
                    nc.scalar.copy(GT[:, HI, f, hf * HALF:(hf + 1) * HALF],
                                   ps[:, (5, 6, 7, 2, 3, 4, 0, 1)[a], 0:HALF]).then_inc(agg_hi, 1)

            with act.Fori(0, NL1) as l:
                mean_layer(l * NT + NT, l * (2 * KT), l * 16 + 64, l * NT + 2 * NREL * NT)
                for n in range(NT):
                    root(l * NT + NT + n + 1, n)
                    x_high(n, l * NT + NT + n + 1)
            block_end(NT + NL1 * NT, NT + NL1 * NT, False)

            X2 = NT + NL1 * NT + NT
            T2 = NT + NL1 * NT
            with act.Fori(0, NL2) as l:
                act.wait_ge(row_in[3], l * 16 + 32)
                act.wait_ge(x_made, l * NT + X2)
                nc.scalar.copy(we_psum, ROW[3][:, :]).then_inc(we_ok, 1)
                w_high(0, l * 16 + 112, l * NT + (2 * NREL + NL1) * NT)
                w_high(1, l * 16 + 112, None)
                with act.Fori(0, PASSES) as i:
                    for k in range(RING):
                        act.wait_ge(ring_free, (l * PASSES + i + PASSES + 1) * RING + k + 1)
                        nc.scalar.activation(Z[:, k % ZR, :], Z[:, k % ZR, :], ACT.Relu).then_inc(z_made, 1)
                for n in range(NT):
                    tr_evac(5 + n % 3, GT, n, l * NT + T2 + n + 1)

                def root_h(o):
                    act.wait_ge(bn_var, l * KT + o + 1)
                    nc.scalar.activation(sd[:, o:o + 1], mv[:, o, 1:2], ACT.Sqrt, bias=epst[:, 0:1])\
                        .then_inc(bn_sd, 1)

                def h_high(o):
                    act.wait_ge(ht_norm, l * KT + o + 1)
                    nc.scalar.activation(XT[:, HI, o, :], HR[:, o, :], ACT.Relu).then_inc(ht_hi, 1)

                act.wait_ge(lcol_made, l + 1)
                for a, (o, hf) in enumerate(HJOBS):
                    act.wait_ge(ht_done, l * (2 * KT) + a + 1)
                    nc.scalar.activation(HR[:, o, hf * HALF:(hf + 1) * HALF], ps[:, HBANKS[a], 0:HALF],
                                         ACT.Identity, bias=lcol[:, 0, o:o + 1]).then_inc(ht_raw, 1)
                    if a >= 2:
                        (h_high if a % 2 else root_h)((a - 2) // 2)
                root_h(KT - 1)
                h_high(KT - 1)
                for n in range(NT):
                    act.wait_ge(xp_made, l * NT + NT + n + 1)
                    nc.scalar.activation(X[:, n, :], X[:, n, :], ACT.Relu).then_inc(x_made, 1)
            block_end(NT + NL1 * NT + NT, X2 + NL2 * NT, True)
            mean_layer(T2 + NL2 * NT, NL1 * 2 * KT, 16 * 11, (2 * NREL + NL1 + NL2) * NT)
            for n in range(NT):
                act.wait_ge(sg_in, n + 1)
                nc.scalar.activation(X[:, n, :], H[:, n, :], ACT.Sigmoid).then_inc(sg_out, 1)
            for n in range(NT):
                root(NT + NL1 * NT + NT + NT + n + 1, n)

        @block.vector
        def _(v):
            chain = Chain(v, dve)
            link = chain.link

            v.memset(B[:, NT - 1, :], 0.0).then_inc(tail_clear, 1)
            v.memset(PAD[:, :, :], 0)
            link(v.memset(one80[:, :], 0.0))
            v.memset(PAD[:, :, 2].bitcast(F32), -1.0).then_inc(pad_made, 1)
            v.memset(zero[:, :], 0.0)
            v.memset(epst[:, :], LN_EPS)

            v.wait_ge(edges_in, 64)
            link(v.tensor_scalar(ti[:, :], e_dst[:, :], 7, None, ALU.arith_shift_right))
            v.tensor_copy(bk[:, :], ti[:, :])
            link(v.tensor_scalar(ti2[:, :], e_dst[:, :], P - 1, None, ALU.bitwise_and))
            v.tensor_copy(REC[:, :, 2].bitcast(F32), ti2[:, :])
            v.tensor_copy(REC[:, :, 0], e_src[:, :])
            link(v.tensor_copy(REC[:, :, 3].bitcast(F32), e_w[:, :]))
            v.scalar_tensor_tensor(out=REC[:, :, 1], in0=e_typ[:, :], scalar=float(NP), in1=e_src[:, :],
                                   op0=ALU.mult, op1=ALU.add)
            for b in range(NT):
                ins = v.tensor_scalar(oh[:, b, :], bk[:, :], float(b), None, ALU.is_equal)
            link(ins)
            for b in range(NT):
                ins = v.tensor_tensor_scan(run[:, b, :], oh[:, b, :], one80[:, :], 0.0, ALU.add, ALU.add)
            ins.then_inc(tot_made, 1)
            v.wait_ge(pre_made, 1)
            link(v.tensor_scalar(basei[:, :], ps[:, 7, NT:2 * NT], float(P - 1), None, ALU.add))
            link(v.tensor_scalar(basei[:, :], basei[:, :], 7, None, ALU.arith_shift_right))
            link(v.tensor_copy(base[:, 0, :], basei[:, :]))
            link(v.memset(base[:, 3, :], 0.0))
            link(v.tensor_tensor_scan(base[:, 1, :], base[:, 0, :], base[:, 3, :], 0.0, ALU.add, ALU.add))
            link(v.tensor_tensor(base[:, 2, :], base[:, 1, :], base[:, 0, :], ALU.subtract))
            link(v.tensor_scalar(base[:, 2, :], base[:, 2, :], float(P), -1.0, ALU.mult, ALU.add))
            ins = v.tensor_tensor(base[:, 3, :], base[:, 2, :], ps[:, 7, 0:NT], ALU.add)
            link(ins)
            v.sem_inc(pre_read, 1)
            for b in range(NT):
                ins = v.scalar_tensor_tensor(out=run[:, b, :], in0=run[:, b, :], scalar=base[0:EP, 3, b:b + 1],
                                             in1=oh[:, b, :], op0=ALU.add, op1=ALU.mult)
            link(ins)
            link(v.tensor_reduce(slot[:, :], run[:, :, :].rearrange("p b c -> p c b"), AX_X, ALU.add))
            link(v.tensor_copy(ti[:, :], slot[:, :]))
            v.tensor_scalar(ti2[:, :], ti[:, :], P - 1, None, ALU.bitwise_and)
            link(v.tensor_scalar(ti[:, :], ti[:, :], 7, None, ALU.arith_shift_right))
            v.scalar_tensor_tensor(out=REC[:, :, 4], in0=ti2[:, :], scalar=float(TE), in1=ti[:, :],
                                   op0=ALU.mult, op1=ALU.add).then_inc(rec_made, 1)
            def tr_low(bank, to, n, count):
                v.wait_ge(tr_hi, count)
                v.tensor_tensor(to[:, LO, :, n * P:(n + 1) * P], ps[:, bank, :].rearrange("p (k m) -> p k m", k=KT),
                                to[:, HI, :, n * P:(n + 1) * P].bitcast(F32), ALU.subtract).then_inc(tr_out, 1)

            def w_low(j, count):
                v.wait_ge(w_hi, count)
                v.tensor_tensor(W[j % 2][:, LO, :, :], WS[j % 2][:, :, :], W[j % 2][:, HI, :, :].bitcast(F32),
                                ALU.subtract).then_inc(w_split, 1)

            def x_low(n, count):
                v.wait_ge(xs_hi, count)
                v.tensor_tensor(XS[:, LO, n, :], X[:, n, :], XS[:, HI, n, :].bitcast(F32),
                                ALU.subtract).then_inc(xs_made, 1)

            for n in range(NT):
                tr_low(n, XT, n, n + 1)
            w_low(0, 1)
            v.wait_ge(consts, 6)
            link(v.tensor_scalar(tf[:, 0, :], iota_t[:, :], base[0:1, 1, 0:1], None, ALU.is_ge))
            for b in range(1, NT - 1):
                link(v.scalar_tensor_tensor(out=tf[:, b % 2, :], in0=iota_t[:, :], scalar=base[0:1, 1, b:b + 1],
                                            in1=tf[:, 1 - b % 2, :], op0=ALU.is_ge, op1=ALU.add))
            of_tile = tf[:, (NT - 2) % 2, :].rearrange("o (g m) -> o g m", m=PACK)
            word = tf[:, 1 - (NT - 2) % 2, 0:TE // PACK]
            link(v.tensor_copy(word, of_tile[:, :, 0]))
            for m in range(1, PACK):
                link(v.scalar_tensor_tensor(out=word, in0=of_tile[:, :, m], scalar=float(BASE ** m), in1=word,
                                            op0=ALU.mult, op1=ALU.add))
            v.tensor_copy(packed[:, :], word).then_inc(bucket_made, 1)

            v.wait_ge(small_in, 48)
            for t in range(NREL):
                ins = v.tensor_scalar(mask[:, t, :], nti[:, :], float(t), None, ALU.is_equal)
            link(v.tensor_scalar(eps1[:, :], eps1[:, :], 1.0, None, ALU.add))
            for t in range(NREL):
                v.wait_ge(row_in[3 + t], 16)
            for q in range(NREL * NT):
                r, n = divmod(q, NT)
                if n == 0:
                    w_low(r + 1, r + 2)
                v.wait_ge(prod_done, q + 1)
                v.wait_ge(row_in[r], 16)
                to = G[q][:, :] if q < RING else X[:, q - RING, :]
                v.tensor_tensor(to, ps[:, (5 + q) % 8, :], ROW[r][:, :], ALU.add).then_inc(prod_out, 1)
                if r == 0:
                    link(v.tensor_scalar(H[:, n, :], ROW[3][:, :], mask[:, 0, n:n + 1], None, ALU.mult))
                else:
                    link(v.scalar_tensor_tensor(out=H[:, n, :], in0=ROW[3 + r][:, :], scalar=mask[:, r, n:n + 1],
                                                in1=H[:, n, :], op0=ALU.mult, op1=ALU.add))
            for q in range(NREL * NT, 2 * NREL * NT):
                t, n = divmod(q - NREL * NT, NT)
                if n == 0 and t < NREL - 1:
                    w_low(NREL + t + 1, NREL + t + 2)
                v.wait_ge(prod_done, q + 1)
                if t:
                    v.wait_ge(prod_out, q - NT + 1)
                v.scalar_tensor_tensor(out=H[:, n, :], in0=ps[:, (5 + q) % 8, :], scalar=mask[:, t, n:n + 1],
                                       in1=H[:, n, :], op0=ALU.mult, op1=ALU.add).then_inc(prod_out, 1)

            v.wait_ge(rec_in, 16)
            link(v.tensor_copy(srcf[:, :], RS[:, :, 0]))
            dl = RS[:, :, 2].bitcast(F32)
            wt = RS[:, :, 3].bitcast(F32)
            v.sem_inc(oh_used, OR)
            with v.Fori(0, PASSES) as i:
                for k in range(RING):
                    v.wait_ge(oh_used, i * RING + k + 1)
                    v.tensor_scalar(SB[k % OR][:, :], iota_h[:, 0:P], dl[:, bass.ds(i * RING + k, 1)], None,
                                    ALU.is_equal)
                    v.tensor_scalar(OS[k % OR][:, :], iota_h[:, :], srcf[:, bass.ds(i * RING + k, 1)], None,
                                    ALU.is_equal).then_inc(oh_made, 1)
            for n in range(NT):
                v.wait_ge(cnt_out, 2 * n + 2)
                link(v.tensor_tensor(rstd[:, n:n + 1], deg[:, 0, n:n + 1], deg[:, 1, n:n + 1], ALU.add))
                link(v.tensor_scalar(rstd[:, n:n + 1], rstd[:, n:n + 1], 1.0, None, ALU.max))
                link(v.reciprocal(rstd[:, n:n + 1], rstd[:, n:n + 1]))
                v.tensor_scalar(AN[:, n, :], AN[:, n, :], rstd[:, n:n + 1], None, ALU.mult)
                v.tensor_scalar(AN_tail[:, n, :], AN_tail[:, n, :], rstd[:, n:n + 1], None, ALU.mult)\
                    .then_inc(adj_made, 1)
            for a in range(NT):
                v.wait_ge(adj_hi, a + 1)
                v.tensor_tensor(AT[:, LO, a, 0:D], ps[:, a, :], AT[:, HI, a, 0:D].bitcast(F32), ALU.subtract)
                v.tensor_tensor(AT[:, LO, a, D:NP], ps[:, 5 + a % 3, 0:P], AT[:, HI, a, D:NP].bitcast(F32),
                                ALU.subtract).then_inc(adj_out, 1)

            v.sem_inc(z_free, ZR)
            with v.Fori(0, PASSES) as i:
                for k in range(RING):
                    v.wait_ge(ring_free, i * RING + k + 1 + RING - ZR)
                    v.tensor_scalar(S[k % ZR][:, :], iota_f[:, :], dl[:, bass.ds(i * RING + k, 1)], None,
                                    ALU.is_equal).then_inc(s_made, 1)

            def stats(rows, n):
                link(v.bn_stats(st[:, n, 0, :], rows))
                v.sem_inc(dve_step, 1)
                v.bn_aggr(mv[:, n, :], st[:, n, 0, :]).then_inc(ln_var, 1)

            def normed(to, rows, n, ln_count):
                v.wait_ge(ln_sd, ln_count)
                link(v.reciprocal(rstd[:, n:n + 1], sd[:, n:n + 1]))
                return v.tensor_scalar(to, rows, mv[:, n, 0:1], rstd[:, n:n + 1], ALU.subtract, ALU.mult)

            for n in range(NT):
                v.wait_ge(acc_done, n + 1)
                link(v.tensor_tensor(H[:, n, :], ps[:, n, :], H[:, n, :], ALU.add))
                link(v.scalar_tensor_tensor(out=H[:, n, :], in0=H[:, n, :], scalar=0.0, in1=B[:, n, :],
                                            op0=ALU.max, op1=ALU.add))
                stats(H[:, n, :], n)
            for n in range(NT):
                normed(X[:, n, :], H[:, n, :], n, n + 1).then_inc(x_made, 1)
                if n:
                    x_low(n - 1, n)
            x_low(NT - 1, NT)

            def mean_parts(tr, agg, w):
                for n in range(NT):
                    tr_low((2 + n) % 5, XT, n, tr + n + 1)
                w_low(0, w + 1)
                w_low(1, w + 2)
                for a in range(2 * KT):
                    f, hf = divmod(a, 2)
                    v.wait_ge(agg_hi, agg + a + 1)
                    v.tensor_tensor(GT[:, LO, f, hf * HALF:(hf + 1) * HALF],
                                    ps[:, (5, 6, 7, 2, 3, 4, 0, 1)[a], 0:HALF],
                                    GT[:, HI, f, hf * HALF:(hf + 1) * HALF].bitcast(F32),
                                    ALU.subtract).then_inc(agg_out, 1)

            def block_end(ln_before):
                for n in range(NT):
                    link(v.tensor_tensor(H[:, n, :], X[:, n, :], B[:, n, :], ALU.add))
                    stats(H[:, n, :], n)
                for n in range(NT):
                    normed(X[:, n, :], H[:, n, :], n, ln_before + n + 1).then_inc(x_made, 1)

            v.wait_ge(b_made, NT)
            PER1 = 6 * NT
            with v.Fori(0, NL1) as l:
                chain.enter(l * PER1)
                mean_parts(l * NT + NT, l * (2 * KT), l * 2 + 6)
                for n in range(NT):
                    v.wait_ge(prod_done, l * NT + 2 * NREL * NT + n + 1)
                    if n == 0:
                        for i in range(3):
                            v.wait_ge(row_in[i], l * 16 + 32)
                    link(v.tensor_tensor(H[:, n, :], ps[:, (5, 6, 7, 0, 1)[n], :], ROW[0][:, :], ALU.add))
                    stats(H[:, n, :], n)
                    link(normed(H[:, n, :], H[:, n, :], n, l * NT + NT + n + 1))
                    link(v.tensor_tensor(H[:, n, :], H[:, n, :], ROW[1][:, :], ALU.mult))
                    link(v.tensor_tensor(H[:, n, :], H[:, n, :], ROW[2][:, :], ALU.add))
                    ins = v.scalar_tensor_tensor(out=X[:, n, :], in0=H[:, n, :], scalar=0.0, in1=X[:, n, :],
                                                 op0=ALU.max, op1=ALU.add)
                    ins.then_inc(x_made, 1)
                    if n:
                        x_low(n - 1, l * NT + NT + n)
                x_low(NT - 1, l * NT + NT + NT)
                chain.leave(PER1, NL1)
            block_end(NT + NL1 * NT)

            v.wait_ge(row_in[4], 32)
            X2 = NT + NL1 * NT + NT
            T2 = NT + NL1 * NT
            for n in range(NT):
                v.wait_ge(x_made, X2 - NT + n + 1)
                v.tensor_tensor(H[:, n, :], X[:, n, :], ROW[4][:, :], ALU.add).then_inc(xp_made, 1)
            v.wait_ge(b_made, 2 * NT)
            PER2 = 6 * KT + NT
            with v.Fori(0, NL2) as l:
                chain.enter(l * PER2)
                v.tensor_copy(lcol[:, :, :], colt[:, :, bass.ds(l, 1), :].rearrange("p a o k -> p a (o k)"))\
                    .then_inc(lcol_made, 1)
                v.wait_ge(we_ok, l + 1)
                v.sem_inc(dve_step, 1)
                w_low(0, l * 2 + 13)
                w_low(1, l * 2 + 14)
                v.wait_ge(w_split, l * 2 + 14)
                v.sem_inc(dve_step, 1)
                with v.Fori(0, PASSES) as i:
                    for k in range(RING):
                        v.wait_ge(z_free, (l * PASSES + i) * RING + k + 1)
                        v.tensor_scalar(S[k % ZR][:, :], iota_f[:, :], dl[:, bass.ds(i * RING + k, 1)], None,
                                        ALU.is_equal).then_inc(s_made, 1)
                        v.wait_ge(gath[k], (l * PASSES + i + PASSES) * 16 + 16)
                        v.scalar_tensor_tensor(out=Z[:, k % ZR, :], in0=we_psum,
                                               scalar=wt[:, bass.ds(i * RING + k, 1)], in1=G[k][:, :],
                                               op0=ALU.mult, op1=ALU.add).then_inc(ring_free, 1)
                v.wait_ge(x_made, l * NT + X2)

                def g(n):
                    v.wait_ge(acc_done, l * NT + NT + n + 1)
                    v.scalar_tensor_tensor(out=H[:, n, :], in0=X[:, n, :], scalar=eps1[:, bass.ds(l, 1)],
                                           in1=ps[:, n, :], op0=ALU.mult, op1=ALU.add).then_inc(g_made, 1)

                for n in range(NT + 2):
                    if n < NT:
                        g(n)
                    if n >= 2:
                        tr_low(5 + (n - 2) % 3, GT, n - 2, l * NT + T2 + n - 1)

                def h_stats(o, hf):
                    v.wait_ge(ht_raw, l * (2 * KT) + HJOBS.index((o, hf)) + 1)
                    link(v.bn_stats(st[:, o, hf, :], HR[:, o, 0:HALF] if hf == 0 else HR[:, o, HALF:N]))

                def h_norm(o):
                    v.wait_ge(bn_sd, l * KT + o + 1)
                    link(v.reciprocal(rstd[:, o:o + 1], sd[:, o:o + 1]))
                    link(v.tensor_tensor(sc[:, 0, o:o + 1], rstd[:, o:o + 1], lcol[:, 1, o:o + 1], ALU.mult))
                    link(v.tensor_tensor(msc[:, o:o + 1], mv[:, o, 0:1], sc[:, 0, o:o + 1], ALU.mult))
                    link(v.tensor_tensor(sc[:, 1, o:o + 1], lcol[:, 2, o:o + 1], msc[:, o:o + 1], ALU.subtract))
                    v.tensor_scalar(HR[:, o, :], HR[:, o, :], sc[:, 0, o:o + 1], sc[:, 1, o:o + 1], ALU.mult,
                                    ALU.add).then_inc(ht_norm, 1)

                def h_low(o):
                    v.wait_ge(ht_hi, l * KT + o + 1)
                    v.scalar_tensor_tensor(out=XT[:, LO, o, :], in0=HR[:, o, :], scalar=0.0,
                                           in1=XT[:, HI, o, :].bitcast(F32), op0=ALU.max,
                                           op1=ALU.subtract).then_inc(ht_out, 1)

                for o in range(KT):
                    h_stats(o, 0)
                    if o:
                        h_norm(o - 1)
                    h_stats(o, 1)
                    v.sem_inc(dve_step, 1)
                    v.bn_aggr(mv[:, o, :], st[:, o, :, :].rearrange("p a s -> p (a s)")).then_inc(bn_var, 1)
                    if o:
                        h_low(o - 1)
                h_norm(KT - 1)
                h_low(KT - 1)
                v.wait_ge(row_in[5], l * 16 + 32)
                v.wait_ge(row_in[4], l * 16 + 48)
                for n in range(NT):
                    v.wait_ge(prod_done, l * NT + (2 * NREL + NL1) * NT + n + 1)
                    link(v.tensor_tensor(X[:, n, :], ps[:, n, :], ROW[5][:, :], ALU.add))
                    v.scalar_tensor_tensor(out=H[:, n, :], in0=X[:, n, :], scalar=0.0, in1=ROW[4][:, :],
                                           op0=ALU.max, op1=ALU.add).then_inc(xp_made, 1)
                chain.leave(PER2, NL2)
            v.wait_ge(x_made, X2 + NL2 * NT)
            block_end(NT + NL1 * NT + NT)

            for n in range(NT):
                x_low(n, NT + NL1 * NT + n + 1)
            mean_parts(T2 + NL2 * NT, NL1 * 2 * KT, 20)
            v.wait_ge(row_in[0], 16 * (NL1 + 2))
            v.wait_ge(b_made, 3 * NT)
            PR3 = (2 * NREL + NL1 + NL2) * NT
            for n in range(NT):
                v.wait_ge(prod_done, PR3 + n + 1)
                v.tensor_tensor(H[:, n, :], ps[:, (5, 6, 7, 0, 1)[n], :], ROW[0][:, :], ALU.add).then_inc(sg_in, 1)
                v.wait_ge(sg_out, n + 1)
                link(v.tensor_tensor(X[:, n, :], X[:, n, :], H[:, n, :], ALU.mult))
                link(v.tensor_tensor(X[:, n, :], X[:, n, :], B[:, n, :], ALU.add))
                stats(X[:, n, :], n)
            for n in range(NT):
                normed(H[:, n, :], X[:, n, :], n, NT + NL1 * NT + NT + NT + n + 1).then_inc(o_made, 1)


def kernel(**inputs):
    import concourse.bacc as _bacc
    from concourse.bass_utils import run_bass_kernel_spmd as _run

    a = {k: np.asarray(v) for k, v in inputs.items()}
    nodes = np.pad(a["node_type_3"], (0, NP - N)).reshape(NT, P).T
    cols = np.stack([a["L2_gnn_" + c].reshape(NL2, KT, P).transpose(2, 0, 1) for c in ("b1", "gamma", "beta")],
                    axis=1)
    again = lambda r: np.concatenate([r, r[:1]])
    pairs = [(a["L1_gnn_W_r"][i].T, a["L1_gnn_W_l"][i].T) for i in range(NL1)]
    pairs += [(a["L2_gnn_W1"][i], a["L2_gnn_W2"][i]) for i in range(NL2)]
    pairs += [(a["L3_gnn_W_r"], a["L3_gnn_W_l"])]
    weights = np.stack([*a["L0_gnn_W_rel"], *a["L0_gnn_W_self"], *(w for p in pairs for w in p)])
    given = {
        "x": a["x"], "src": a["src"].reshape(EP, EC), "dst": a["dst"].reshape(EP, EC),
        "etype": a["edge_type_3"].reshape(EP, EC), "ew": a["edge_weight1"].reshape(EP, EC), "ntype": nodes,
        "weights": weights, "b_rel": a["L0_gnn_b_rel"], "b_self": a["L0_gnn_b_self"],
        "b1_l1": a["L1_gnn_b"], "ln_g": a["L1_gnn_ln_g"], "ln_b": a["L1_gnn_ln_b"],
        "eps": a["L2_gnn_eps"].reshape(1, NL2), "we": again(a["L2_gnn_We"].reshape(NL2, D)),
        "be": again(a["L2_gnn_be"]), "cols": cols,
        "b2": a["L2_gnn_b2"], "b3": a["L3_gnn_b"].reshape(1, D),
    }
    nc = _bacc.Bacc("TRN2", target_bir_lowering=False, num_devices=1)
    arrays, args = {}, []
    for name, v in given.items():
        arrays[f"in_{name}"] = np.ascontiguousarray(v)
        args.append(nc.dram_tensor(f"in_{name}", v.shape, mybir.dt.from_np(v.dtype), kind="ExternalInput").ap())
    args.append(nc.dram_tensor("out_0", (N, D), F32, kind="ExternalOutput").ap())
    build(nc, *args)
    return _run(nc, [arrays], core_ids=[0]).results[0]["out_0"]
```

```python
from contextlib import ExitStack

import numpy as np

import concourse.bass as bass
from concourse import mybir

ALU = mybir.AluOpType
ACT = mybir.ActivationFunctionType
AX_X = mybir.AxisListType.X
F32 = mybir.dt.float32
F16 = mybir.dt.float16
BF16 = mybir.dt.bfloat16
F32R = mybir.dt.float32r
I32 = mybir.dt.int32

P = 128
N = 625
D = 512
E = 10000
NT = -(-N // P)
NP = NT * P
LAST = N - (NT - 1) * P
KT = D // P
HALF = NP // 2
EP = 125
EC = E // EP
RING = 12
GRP = 2
TE = -(-((E - NT) // P + NT) // RING) * RING
PASSES = TE // RING
PACK = 6
BITS = 3
BASE = 1 << BITS
OR = 6
ZR = 4
RECW = 5
HJOBS = ((0, 0), (1, 0), (0, 1), (1, 1), (2, 0), (2, 1), (3, 0), (3, 1))
HBANKS = (0, 1, 2, 3, 4, 7, 5, 6)
KGROUPS = (*((k,) for k in range(KT - 2)), (KT - 2, KT - 1))
HI, LO = 0, 1
THREE = ((HI, HI), (HI, LO), (LO, HI))
LN_EPS = 1e-5
NREL = 3
LAST_L = [max(2 * n, 1) for n in range(NT)]
LAST_E = [min(2 * n + 3, 2 * NT) for n in range(NT)]
TRJOBS = NT + 2
NL1 = 3
NL2 = 4


class Chain:

    def __init__(self, eng, sem):
        self.eng, self.sem, self.n, self.reg = eng, sem, 0, None

    def link(self, ins):
        self.n += 1
        ins.then_inc(self.sem, 1)
        self.eng.wait_ge(self.sem, self.n if self.reg is None else self.reg + self.n)

    def enter(self, reg_part):
        self.reg, self.start = reg_part, self.n

    def leave(self, per, times):
        assert self.n - self.start == per, (self.n - self.start, per)
        self.reg = None
        self.n = self.start + per * times


def build(nc, x, src, dst, etype, ew, ntype, weights, b_rel, b_self, b1_l1, ln_g, ln_b,
          eps, we, be, cols, b2, b3, out):
    rec_d = nc.dram_tensor("edge_records", (P * TE, 4), I32).ap()
    xr_d = nc.dram_tensor("rel_rows", (NREL * NP, D), F32).ap()
    xg_d = nc.dram_tensor("gine_rows", (NP, D), F32).ap()

    with ExitStack() as ctx:
        def sb(name, shape, dt=F32):
            return ctx.enter_context(nc.sbuf_tensor(name, shape, dt))

        def sem(name):
            return ctx.enter_context(nc.semaphore(name))

        B = sb("block_in", [P, NT, D])
        X = sb("x_cur", [P, NT, D])
        H = sb("work", [P, NT, D])
        XT = sb("xT", [P, 2, KT, NP], F32R)
        GT = sb("gT", [P, 2, KT, NP], F32R)
        HR = H[:, :, :].rearrange("p t d -> p (t d)").rearrange("p (k n) -> p k n", k=KT)
        AT = sb("adjT", [P, 2, NT, NP], F32R)
        AN = X
        AN_tail = sb("adj_tail", [P, NT, P])
        W = [sb(f"w{i}", [P, 2, KT, D], F32R) for i in range(2)]
        ROW = [sb(f"row{i}", [P, D]) for i in range(6)]
        Z = sb("edge_rows", [P, ZR, D])
        assert ZR == KT
        WS = [sb("w_stage", [P, KT, D]), Z]
        S = [sb(f"onehot_dst{i}", [P, P]) for i in range(ZR)]
        SB = [sb(f"onehot_dst_b{i}", [P, P], BF16) for i in range(OR)]
        OS = [sb(f"onehot_src{i}", [P, NP], BF16) for i in range(OR)]
        RS = sb("records", [P, TE, 4], I32)
        srcf = sb("srcf", [P, TE])
        packed = sb("buckets_packed", [1, TE // PACK], I32)
        e_dst = sb("e_dst", [EP, EC], I32)
        e_src = sb("e_src", [EP, EC], I32)
        e_typ = sb("e_typ", [EP, EC], I32)
        e_w = sb("e_w", [EP, EC])
        REC = sb("rec_sb", [EP, EC, RECW], I32)
        PAD = RS
        ti = sb("ti", [EP, EC], I32)
        ti2 = sb("ti2", [EP, EC], I32)
        bk = sb("bk", [EP, EC])
        oh = sb("oh", [EP, NT, EC])
        run = sb("run", [EP, NT, EC])
        scan_zero = sb("scan_zero", [EP, EC])
        slot = sb("slot", [EP, EC])
        tri = sb("tri", [EP, P])
        ones = sb("ones", [EP, P])
        base = sb("base", [P, 4, NT])
        basei = sb("basei", [P, NT], I32)
        tf = H[0:1, :, :].rearrange("o t d -> o (t d)")[:, 0:2 * TE].rearrange("o (a t) -> o a t", a=2)
        iota_f = sb("iota_f", [P, P])
        iota_h = sb("iota_h", [P, NP], F16)
        iota_t = sb("iota_t", [1, TE])
        ident = sb("ident", [P, P])
        zero = sb("zero", [P, D], BF16)
        epst = sb("epst", [P, 1])
        nti = sb("nti", [P, NT], I32)
        mask = sb("mask", [P, NREL, NT])
        eps1 = sb("eps1", [P, NL2])
        colt = sb("colt", [P, 3, NL2, KT])
        lcol = sb("lcol", [P, 3, KT])
        st = sb("st", [P, NT, 2, 6])
        msc = sb("msc", [P, KT])
        mv = sb("mv", [P, NT, 2])
        sd = sb("sd", [P, NT])
        rstd = sb("rstd", [P, NT])
        deg = sb("deg", [P, 2, NT])
        sc = sb("sc", [P, 2, KT])
        with ExitStack() as ring:
            G = [ring.enter_context(nc.sbuf_tensor(f"gathered{i}", [P, D], F32)) for i in range(RING)]
        XS = sb("x_parts", [P, 2, NT, D], F32R)
        ps = ctx.enter_context(nc.psum_tensor("ps", [P, 8, D], F32))
        ps_tail = ps[:, 5:7, :].rearrange("p a n -> p (a n)")

        def adj_part(part, a):
            bank = ps[:, 5 + a % 3, :]
            if a < NT:
                return AT[:, part, 0:KT, a * P:(a + 1) * P], bank.rearrange("p (c d) -> p c d", d=P)
            if a == NT:
                return AT[:, part, KT, 0:D], bank
            return AT[:, part, KT, D:NP], bank[:, 0:P]

        consts = sem("consts")
        tri0 = sem("tri0")
        edges_in = sem("edges_in")
        small_in = sem("small_in")
        x_in = sem("x_in")
        tail_clear = sem("tail_clear")
        pad_made = sem("pad_made")
        pad_out = sem("pad_out")
        ws_in = [sem(f"w_stage{i}_in") for i in range(2)]
        w_hi = sem("w_hi")
        w_split = sem("w_split")
        xs_hi = sem("xs_hi")
        sum_made = sem("sum_made")
        xs_made = sem("xs_made")
        row_in = [sem(f"row{i}_in") for i in range(6)]
        dve = sem("dve_chain")
        dve_step = sem("dve_step")
        lcol_made = sem("lcol_made")
        tot_made = sem("tot_made")
        pre_made = sem("pre_made")
        pre_read = sem("pre_read")
        rec_made = sem("rec_made")
        scat = sem("scattered")
        sp_step = sem("sp_step")
        pool_step = sem("pool_step")
        rec_in = sem("rec_in")
        bucket_made = sem("bucket_made")
        oh_made = sem("onehots_made")
        oh_used = sem("onehots_used")
        cnt_done = sem("counts_done")
        cnt_out = sem("counts_out")
        deg_made = sem("degrees_made")
        adj_scaled = sem("adj_scaled")
        adj_tr = sem("adj_tr")
        adj_hi = sem("adj_hi")
        adj_out = sem("adj_out")
        tr_done = sem("tr_done")
        tr_hi = sem("tr_hi")
        tr_out = sem("tr_out")
        prod_done = sem("prod_done")
        prod_out = sem("prod_out")
        xr_out = sem("xr_out")
        ring_free = sem("ring_free")
        gath = [sem(f"gath{i}") for i in range(RING)]
        s_made = sem("onehot_made")
        z_free = sem("z_free")
        z_made = sem("z_relu")
        acc_done = sem("acc_done")
        x_made = sem("x_made")
        b_made = sem("b_made")
        ln_var = sem("ln_var")
        ln_sd = sem("ln_sd")
        agg_done = sem("agg_done")
        agg_hi = sem("agg_hi")
        agg_out = sem("agg_out")
        we_ok = sem("we_ok")
        xp_made = sem("xp_made")
        xg_out = sem("xg_out")
        g_made = sem("g_made")
        ht_done = sem("ht_done")
        ht_raw = sem("ht_raw")
        bn_var = sem("bn_var")
        bn_sd = sem("bn_sd")
        ht_norm = sem("ht_norm")
        ht_hi = sem("ht_hi")
        ht_out = sem("ht_out")
        sg_in = sem("sg_in")
        sg_out = sem("sg_out")
        o_made = sem("o_made")
        o_out = sem("o_out")
        we_psum = ps[:, 5, :]

        xv = [x[n * P:min(N, n * P + P), :] for n in range(NT)]
        block = ctx.enter_context(nc.Block())

        @block.sync
        def _(sp):
            def w_load(j):
                sp.dma_start(WS[j % 2][:, :, :], weights[j].rearrange("(k p) n -> p k n", p=P))\
                    .then_inc(ws_in[j % 2], 16)

            def w_load_of(l, j):
                sp.dma_start(WS[j % 2][:, :, :],
                             weights[bass.ds(2 * l + j, 1), :, :].rearrange("o (k p) n -> p (o k) n", p=P))\
                    .then_inc(ws_in[j % 2], 16)

            def row_load(i, r):
                sp.dma_start(ROW[i][:, :], r.broadcast_to([P, D])).then_inc(row_in[i], 16)

            for t, d in ((e_dst, dst), (e_src, src), (e_typ, etype), (e_w, ew)):
                sp.dma_start(t[:, :], d).then_inc(edges_in, 16)
            for n in range(NT - 1):
                sp.dma_start(B[:, n, :], xv[n]).then_inc(x_in, 16)
            sp.wait_ge(tail_clear, 1)
            sp.dma_start(B[0:LAST, NT - 1, :], xv[NT - 1]).then_inc(x_in, 16)
            sp.wait_ge(pad_made, 1)
            sp.dma_start(rec_d.rearrange("(p t) r -> p t r", p=P), PAD[:, :, :]).then_inc(pad_out, 16)
            w_load(0)
            w_load(1)
            sp.dma_start(nti[:, :], ntype).then_inc(small_in, 16)
            sp.dma_start(eps1[:, :], eps.broadcast_to([P, NL2])).then_inc(small_in, 16)
            sp.dma_start(colt[:, :, :, :], cols).then_inc(small_in, 16)
            for r in range(NREL):
                row_load(r, b_rel[r:r + 1, :])
                row_load(3 + r, b_self[r:r + 1, :])
            for j in (2, 3):
                sp.wait_ge(w_split, j - 1)
                w_load(j)
            for q in range(NREL * NT):
                sp.wait_ge(prod_out, q + 1)
                r, n = divmod(q, NT)
                rows = G[q] if q < RING else X[:, q - RING]
                sp.dma_start(xr_d[r * NP + n * P:r * NP + (n + 1) * P, :], rows[:, :] if q < RING else rows)\
                    .then_inc(xr_out, 16)
            for j in (4, 5):
                sp.wait_ge(w_split, j - 1)
                w_load(j)
            sp.wait_ge(scat, 16 * EC)
            sp.dma_start(RS[:, :, :], rec_d.rearrange("(p t) r -> p t r", p=P)).then_inc(rec_in, 16)

            for j in (6, 7):
                sp.wait_ge(w_split, j - 1)
                w_load(j)
            with sp.Fori(0, NL1) as l:
                sp.wait_ge(x_made, l * NT + NT)
                sp.sem_inc(sp_step, 1)
                for i, r in ((0, b1_l1), (1, ln_g), (2, ln_b)):
                    sp.dma_start(ROW[i][:, :], r[bass.ds(l, 1), :].broadcast_to([P, D])).then_inc(row_in[i], 16)
                for j in (0, 1):
                    sp.wait_ge(w_split, 2 * l + 7 + j)
                    sp.sem_inc(sp_step, 1)
                    w_load_of(l, 8 + j)
            row_load(3, we[0:1, :])
            row_load(4, be[0:1, :])
            with sp.Fori(0, NL2) as l:
                for n in range(NT):
                    sp.wait_ge(xp_made, l * NT + n + 1)
                    sp.dma_start(xg_d[n * P:(n + 1) * P, :], H[:, n, :]).then_inc(xg_out, 16)
                sp.dma_start(ROW[5][:, :], b2[bass.ds(l, 1), :].broadcast_to([P, D])).then_inc(row_in[5], 16)
                sp.dma_start(ROW[4][:, :], be[bass.ds(l + 1, 1), :].broadcast_to([P, D])).then_inc(row_in[4], 16)
                sp.wait_ge(we_ok, l + 1)
                sp.sem_inc(sp_step, 1)
                sp.dma_start(ROW[3][:, :], we[bass.ds(l + 1, 1), :].broadcast_to([P, D])).then_inc(row_in[3], 16)
                sp.wait_ge(w_split, 2 * l + 13)
                sp.sem_inc(sp_step, 1)
                w_load_of(l, 14)
                sp.wait_ge(acc_done, l * NT + 2 * NT)
                sp.sem_inc(sp_step, 1)
                w_load_of(l, 15)
            row_load(0, b3)
            for n in range(NT):
                sp.wait_ge(o_made, n + 1)
                rows = P if n < NT - 1 else LAST
                sp.dma_start(out[n * P:n * P + rows, :], H[0:rows, n, :]).then_inc(o_out, 16)
            sp.wait_ge(o_out, 16 * NT)
            sp.wait_ge(row_in[3], 16 * (NL2 + 2))
            sp.wait_ge(row_in[4], 16 * (NL2 + 2))

        @block.gpsimd
        def _(gp):
            gp.memset(tri[:, :], 1.0).then_inc(tri0, 1)
            gp.memset(ident[:, :], 0.0).then_inc(tri0, 1)
            gp.memset(ones[:, :], 1.0).then_inc(consts, 1)
            gp.wait_ge(tri0, 2)
            gp.affine_select(out=tri[:, :], in_=tri[:, :], compare_op=ALU.is_gt, fill=0.0, base=0,
                             pattern=[[1, P]], channel_multiplier=-1).then_inc(consts, 1)
            gp.affine_select(out=ident[:, :], in_=ident[:, :], compare_op=ALU.not_equal, fill=1.0, base=0,
                             pattern=[[-1, P]], channel_multiplier=1).then_inc(consts, 1)
            gp.iota(iota_f[:, :], [[1, P]], base=0, channel_multiplier=0,
                    allow_small_or_imprecise_dtypes=True).then_inc(consts, 1)
            gp.iota(iota_h[:, :], [[1, NP]], base=0, channel_multiplier=0,
                    allow_small_or_imprecise_dtypes=True).then_inc(consts, 1)
            gp.iota(iota_t[:, :], [[1, TE]], base=0, channel_multiplier=0,
                    allow_small_or_imprecise_dtypes=True).then_inc(consts, 1)

            gp.wait_ge(pad_out, 16)
            gp.wait_ge(rec_made, 1)
            for c in range(EC):
                gp.indirect_dma_start(rec_d, bass.IndirectOffsetOnAxis(ap=REC[:, c, 4:5], axis=0),
                                      REC[:, c, 0:4], None).then_inc(scat, 16)

            def gather(table, column, used):
                for t in range(TE):
                    if t % GRP == 0:
                        gp.wait_ge(ring_free, used + t + GRP)
                        gp.sem_inc(pool_step, 1)
                    gp.indirect_dma_start(G[t % RING][:, :], None, table,
                                          bass.IndirectOffsetOnAxis(ap=RS[:, t, column:column + 1], axis=0))\
                        .then_inc(gath[t % RING], 16)

            gp.sem_inc(ring_free, RING)
            gp.wait_ge(rec_in, 16)
            gp.wait_ge(xr_out, 16 * NREL * NT)
            gather(xr_d, 1, 0)

            def x_lows(count):
                for n in range(NT):
                    gp.wait_ge(xs_hi, count + n + 1)
                    gp.sem_inc(pool_step, 1)
                    gp.tensor_tensor(XS[:, LO, n, :], X[:, n, :], XS[:, HI, n, :].bitcast(F32),
                                     ALU.subtract).then_inc(xs_made, 1)

            x_lows(0)
            with gp.Fori(0, NL1 - 1) as l:
                x_lows(l * NT + NT)
            X2 = NT + NL1 * NT + NT
            for n in range(NT):
                gp.wait_ge(x_made, NL1 * NT + LAST_L[n])
                gp.tensor_tensor(H[:, n, :], X[:, n, :], B[:, n, :], ALU.add).then_inc(sum_made, 1)
            with gp.Fori(0, NL2) as l:
                gp.wait_ge(xg_out, (l + 1) * (16 * NT))
                gp.sem_inc(pool_step, 1)
                gather(xg_d, 0, l * TE + TE)
            for n in range(NT):
                gp.wait_ge(x_made, X2 + NL2 * NT - NT + n + 1)
                gp.tensor_tensor(H[:, n, :], X[:, n, :], B[:, n, :], ALU.add).then_inc(sum_made, 1)
            x_lows(NL1 * NT)

        @block.tensor
        def _(pe):
            def transposes(bank, rows):
                for k in range(KT):
                    mm = pe.transpose(ps[:, bank, k * P:(k + 1) * P], rows[:, k * P:(k + 1) * P], ident[:, :])
                mm.then_inc(tr_done, 1)

            def natural(bank, lt, w, n, first=True, last=True):
                for k in range(KT):
                    for a, b in THREE:
                        mm = pe.matmul(ps[:, bank, :], lt[:, a, k, n * P:(n + 1) * P], w[:, b, k, :],
                                       start=first and k == 0 and (a, b) == THREE[0],
                                       stop=last and k == KT - 1 and (a, b) == THREE[-1])
                return mm

            def zeros(bank, open_):
                return pe.matmul(ps[:, bank, :], zero[:, 0:P], zero[:, :], start=open_, stop=not open_)

            def buckets(i, k):
                word = pe.value_load(packed[0:1, bass.ds(i * (RING // PACK) + k // PACK, 1)],
                                     min_val=0, max_val=BASE ** PACK - 1)
                return [pe.snap((word >> (BITS * m)) & (BASE - 1), min_val=0, max_val=NT - 1) for m in range(PACK)]

            pe.wait_ge(consts, 6)
            pe.wait_ge(tot_made, 1)
            tot = run[:, :, EC - 1]
            pe.matmul(ps[:, 7, 0:NT], tri[:, :], tot, start=True, stop=True)
            pe.matmul(ps[:, 7, NT:2 * NT], ones[:, :], tot, start=True, stop=True).then_inc(pre_made, 1)
            pe.wait_ge(x_in, 16 * NT)
            for n in range(NT):
                transposes(n, B[:, n, :])
            for q in range(2 * NREL * NT):
                j, n = divmod(q, NT)
                if j == 0:
                    pe.wait_ge(tr_out, n + 1)
                if n == 0:
                    pe.wait_ge(w_split, j + 1)
                if q == 2:
                    pe.wait_ge(pre_read, 1)
                if q >= 8:
                    pe.wait_ge(prod_out, q - 7)
                natural((5 + q) % 8, XT, W[j % 2], n).then_inc(prod_done, 1)
            pe.wait_ge(prod_out, 2 * NREL * NT)
            pe.wait_ge(bucket_made, 1)
            for b in range(7):
                zeros(b, True)
            with pe.Fori(0, PASSES) as i:
                for k in range(RING):
                    if k % PACK == 0:
                        banks = buckets(i, k)
                    b = banks[k % PACK]
                    if k % (OR // 2) == 0:
                        pe.wait_ge(oh_made, i * RING + k + OR // 2)
                    pe.matmul(ps[:, b, :], SB[k % OR][:, :], OS[k % OR][:, 0:D],
                              start=False, stop=False, skip_group_check=True)
                    pe.matmul(ps_tail[:, bass.ds(b * P, P)], SB[k % OR][:, :], OS[k % OR][:, D:NP],
                              start=False, stop=False, skip_group_check=True).then_inc(oh_used, 1)
            for b in range(7):
                mm = zeros(b, False)
            mm.then_inc(cnt_done, 1)
            for b in range(NT):
                pe.wait_ge(cnt_out, b + 1)
                zeros(b, True)
            with pe.Fori(0, PASSES) as i:
                for k in range(RING):
                    if k % PACK == 0:
                        banks = buckets(i, k)
                    b = banks[k % PACK]
                    if k % 2 == 0:
                        pe.wait_ge(gath[k], i * 16 + 16)
                        pe.wait_ge(gath[k + 1], i * 16 + 16)
                        pe.wait_ge(s_made, i * RING + k + 2)
                    pe.matmul(ps[:, b, :], S[k % ZR][:, :], G[k][:, :],
                              start=False, stop=False, skip_group_check=True).then_inc(ring_free, 1)
            for b in range(NT):
                zeros(b, False).then_inc(acc_done, 1)
            for a in range(TRJOBS):
                if a < NT:
                    pe.wait_ge(adj_scaled, a + 1)
                if a >= 3:
                    pe.wait_ge(adj_out, a - 2)
                for c in range(KT if a < TRJOBS - 1 else 1):
                    if a < NT:
                        i = AN[:, a, c * P:(c + 1) * P]
                    else:
                        i = AN_tail[:, c if a == NT else NT - 1, :]
                    mm = pe.transpose(ps[:, 5 + a % 3, c * P:(c + 1) * P], i, ident[:, :])
                mm.then_inc(adj_tr, 1)

            def mean_layer(l, last_x, wcount):
                for n in range(NT):
                    pe.wait_ge(x_made, last_x + n + 1)
                    if n + 2 < NT:
                        pe.wait_ge(ln_var, n + 3)
                    transposes((2 + n) % 5, X[:, n, :])
                for a in range(2 * KT):
                    f, hf = divmod(a, 2)
                    if a == 0:
                        pe.wait_ge(adj_out, TRJOBS)
                    if a >= 3:
                        pe.wait_ge(tr_out, wcount["tr"] + a - 2)
                    for n in range(NT):
                        if a == 0:
                            pe.wait_ge(xs_made, wcount["xs"] + n + 1)
                        for p, q in THREE:
                            mm = pe.matmul(ps[:, (5, 6, 7, 2, 3, 4, 0, 1)[a], 0:HALF],
                                           XS[:, p, n, f * P:(f + 1) * P],
                                           AT[:, q, n, hf * HALF:(hf + 1) * HALF],
                                           start=n == 0 and (p, q) == THREE[0],
                                           stop=n == NT - 1 and (p, q) == THREE[-1])
                    mm.then_inc(agg_done, 1)
                pe.wait_ge(tr_out, wcount["tr"] + NT)
                for n in range(NT):
                    if n == 0:
                        pe.wait_ge(agg_out, wcount["agg"] + 3)
                        pe.wait_ge(w_split, wcount["w"] + 1)
                    if n == 3:
                        pe.wait_ge(agg_out, wcount["agg"] + 2 * KT)
                    natural((5, 6, 7, 0, 1)[n], XT, W[0], n, last=False)
                    if n == 0:
                        pe.wait_ge(agg_out, wcount["agg"] + 2 * KT)
                        pe.wait_ge(w_split, wcount["w"] + 2)
                    natural((5, 6, 7, 0, 1)[n], GT, W[1], n, first=False).then_inc(prod_done, 1)

            with pe.Fori(0, NL1) as l:
                mean_layer(l, l * NT, {"tr": l * NT + NT, "agg": l * (2 * KT), "w": l * 2 + 6, "xs": l * NT})

            T2 = NT + NL1 * NT
            X2 = NT + NL1 * NT + NT
            with pe.Fori(0, NL2) as l:
                pe.wait_ge(x_made, l * NT + X2)
                for b in range(NT):
                    zeros(b, True)
                with pe.Fori(0, PASSES) as i:
                    for k in range(RING):
                        if k % PACK == 0:
                            banks = buckets(i, k)
                        b = banks[k % PACK]
                        if k % 2 == 0:
                            pe.wait_ge(s_made, (l * PASSES + i + PASSES) * RING + k + 2)
                            pe.wait_ge(z_made, (l * PASSES + i) * RING + k + 2)
                        pe.matmul(ps[:, b, :], S[k % ZR][:, :], Z[:, k % ZR, :],
                                  start=False, stop=False, skip_group_check=True).then_inc(z_free, 1)
                for b in range(NT):
                    zeros(b, False).then_inc(acc_done, 1)
                for n in range(NT):
                    pe.wait_ge(g_made, l * NT + n + 1)
                    transposes(n, H[:, n, :])
                pe.wait_ge(w_split, l * 2 + 13)
                for a, (o, hf) in enumerate(HJOBS):
                    if a == 0:
                        pe.wait_ge(tr_out, l * NT + T2 + 3)
                    if a == 2:
                        pe.wait_ge(tr_out, l * NT + T2 + NT)
                    for k in range(KT):
                        for p, q in THREE:
                            mm = pe.matmul(ps[:, HBANKS[a], 0:HALF],
                                           W[0][:, p, k, o * P:(o + 1) * P],
                                           GT[:, q, k, hf * HALF:(hf + 1) * HALF],
                                           start=k == 0 and (p, q) == THREE[0],
                                           stop=k == KT - 1 and (p, q) == THREE[-1])
                    mm.then_inc(ht_done, 1)
                pe.wait_ge(w_split, l * 2 + 14)
                pe.wait_ge(ht_raw, l * (2 * KT) + NT)
                for group in KGROUPS:
                    for n in range(NT):
                        for k in group:
                            if n == 0:
                                pe.wait_ge(ht_out, l * KT + k + 1)
                            for p, q in THREE:
                                mm = pe.matmul(ps[:, n, :], XT[:, p, k, n * P:(n + 1) * P], W[1][:, q, k, :],
                                               start=k == 0 and (p, q) == THREE[0],
                                               stop=k == KT - 1 and (p, q) == THREE[-1])
                        if k == KT - 1:
                            mm.then_inc(prod_done, 1)

            mean_layer(NL1, X2 + NL2 * NT,
                       {"tr": T2 + NL2 * NT, "agg": NL1 * 2 * KT, "w": 20, "xs": NL1 * NT})

        @block.scalar
        def _(act):
            def tr_evac(bank, to, n, count):
                act.wait_ge(tr_done, count)
                nc.scalar.copy(to[:, HI, :, n * P:(n + 1) * P],
                               ps[:, bank, :].rearrange("p (k m) -> p k m", k=KT)).then_inc(tr_hi, 1)

            def w_high(j, landed, done):
                act.wait_ge(ws_in[j % 2], landed)
                if done is not None:
                    act.wait_ge(prod_done, done)
                for k in range(KT):
                    ins = nc.scalar.copy(W[j % 2][:, HI, k, :], WS[j % 2][:, k, :])
                ins.then_inc(w_hi, 1)

            def x_high(n, count):
                act.wait_ge(x_made, count)
                nc.scalar.copy(XS[:, HI, n, :], X[:, n, :]).then_inc(xs_hi, 1)

            def root(count, n):
                act.wait_ge(ln_var, count)
                nc.scalar.activation(sd[:, n:n + 1], mv[:, n, 1:2], ACT.Sqrt, bias=epst[:, 0:1])\
                    .then_inc(ln_sd, 1)

            tr_evac(0, XT, 0, 1)
            w_high(0, 16, None)
            for n in range(1, NT):
                tr_evac(n, XT, n, n + 1)
            for j in range(1, 2 * NREL):
                w_high(j, 16 * (j // 2 + 1), NT * (j - 1) if j >= 2 else None)
            act.wait_ge(cnt_done, 1)
            for b in range(NT):
                nc.scalar.activation(AN[:, b, 0:D], ps[:, b, :], ACT.Copy, accum_out=deg[:, 0, b:b + 1])\
                    .then_inc(cnt_out, 1)
            for b in range(NT):
                nc.scalar.activation(AN_tail[:, b, :], ps_tail[:, b * P:(b + 1) * P], ACT.Copy,
                                     accum_out=deg[:, 1, b:b + 1]).then_inc(cnt_out, 1)
            act.wait_ge(deg_made, 1)
            for n in range(NT):
                nc.scalar.activation(AN[:, n, :], AN[:, n, :], ACT.Identity, scale=rstd[:, n:n + 1])
                nc.scalar.activation(AN_tail[:, n, :], AN_tail[:, n, :], ACT.Identity, scale=rstd[:, n:n + 1])\
                    .then_inc(adj_scaled, 1)

            def block_end(ln_before, x_before, adj=False):
                for n in range(TRJOBS if adj else NT + 1):
                    if adj:
                        act.wait_ge(adj_tr, n + 1)
                        to, of = adj_part(HI, n)
                        nc.scalar.copy(to, of).then_inc(adj_hi, 1)
                    if n < NT:
                        root(ln_before + n + 1, n)
                    if 1 <= n <= NT:
                        x_high(n - 1, x_before + n)
                        nc.scalar.copy(B[:, n - 1, :], X[:, n - 1, :]).then_inc(b_made, 1)

            block_end(0, 0, adj=True)

            def mean_layer(tr, agg, landed, done):
                for n in range(NT):
                    tr_evac((2 + n) % 5, XT, n, tr + n + 1)
                w_high(0, landed, done)
                w_high(1, landed, None)
                for a in range(2 * KT):
                    f, hf = divmod(a, 2)
                    act.wait_ge(agg_done, agg + a + 1)
                    nc.scalar.copy(GT[:, HI, f, hf * HALF:(hf + 1) * HALF],
                                   ps[:, (5, 6, 7, 2, 3, 4, 0, 1)[a], 0:HALF]).then_inc(agg_hi, 1)

            with act.Fori(0, NL1 - 1) as l:
                mean_layer(l * NT + NT, l * (2 * KT), l * 16 + 64, l * NT + 2 * NREL * NT)
                for n in range(NT):
                    root(l * NT + NT + n + 1, n)
                    x_high(n, l * NT + NT + n + 1)
            l = NL1 - 1
            mean_layer(l * NT + NT, l * (2 * KT), l * 16 + 64, l * NT + 2 * NREL * NT)
            for n in range(NT + 1):
                if n < NT:
                    root(NL1 * NT + LAST_L[n], n)
                if n:
                    root(NL1 * NT + LAST_E[n - 1], n - 1)
                    act.wait_ge(x_made, NL1 * NT + LAST_E[n - 1])
                    nc.scalar.copy(B[:, n - 1, :], X[:, n - 1, :]).then_inc(b_made, 1)

            X2 = NT + NL1 * NT + NT
            T2 = NT + NL1 * NT
            with act.Fori(0, NL2) as l:
                act.wait_ge(row_in[3], l * 16 + 32)
                act.wait_ge(x_made, l * NT + X2)
                nc.scalar.copy(we_psum, ROW[3][:, :]).then_inc(we_ok, 1)
                w_high(0, l * 16 + 112, l * NT + (2 * NREL + NL1) * NT)
                w_high(1, l * 16 + 112, None)
                with act.Fori(0, PASSES) as i:
                    for k in range(RING):
                        act.wait_ge(ring_free, (l * PASSES + i + PASSES + 1) * RING + k + 1)
                        nc.scalar.activation(Z[:, k % ZR, :], Z[:, k % ZR, :], ACT.Relu).then_inc(z_made, 1)
                for n in range(NT):
                    tr_evac(n, GT, n, l * NT + T2 + n + 1)

                def root_h(o):
                    act.wait_ge(bn_var, l * KT + o + 1)
                    nc.scalar.activation(sd[:, o:o + 1], mv[:, o, 1:2], ACT.Sqrt, bias=epst[:, 0:1])\
                        .then_inc(bn_sd, 1)

                def h_high(o):
                    act.wait_ge(ht_norm, l * KT + o + 1)
                    nc.scalar.activation(XT[:, HI, o, :], HR[:, o, :], ACT.Relu).then_inc(ht_hi, 1)

                act.wait_ge(lcol_made, l + 1)
                for a, (o, hf) in enumerate(HJOBS):
                    act.wait_ge(ht_done, l * (2 * KT) + a + 1)
                    nc.scalar.activation(HR[:, o, hf * HALF:(hf + 1) * HALF], ps[:, HBANKS[a], 0:HALF],
                                         ACT.Identity, bias=lcol[:, 0, o:o + 1]).then_inc(ht_raw, 1)
                    if a >= 2:
                        (h_high if a % 2 else root_h)((a - 2) // 2)
                root_h(KT - 1)
                h_high(KT - 1)
                for n in range(NT):
                    act.wait_ge(xp_made, l * NT + NT + n + 1)
                    nc.scalar.activation(X[:, n, :], X[:, n, :], ACT.Relu).then_inc(x_made, 1)
            block_end(NT + NL1 * NT + NT, X2 + NL2 * NT)
            mean_layer(T2 + NL2 * NT, NL1 * 2 * KT, 16 * 11, (2 * NREL + NL1 + NL2) * NT)
            for n in range(NT):
                act.wait_ge(sg_in, n + 1)
                nc.scalar.activation(X[:, n, :], H[:, n, :], ACT.Sigmoid).then_inc(sg_out, 1)
            for n in range(NT):
                root(NT + NL1 * NT + NT + NT + n + 1, n)

        @block.vector
        def _(v):
            chain = Chain(v, dve)
            link = chain.link

            v.memset(B[:, NT - 1, :], 0.0).then_inc(tail_clear, 1)
            v.memset(PAD[:, :, :], 0)
            link(v.memset(scan_zero[:, :], 0.0))
            v.memset(PAD[:, :, 2].bitcast(F32), -1.0).then_inc(pad_made, 1)
            v.memset(zero[:, :], 0.0)
            v.memset(epst[:, :], LN_EPS)

            v.wait_ge(edges_in, 64)
            link(v.tensor_scalar(ti[:, :], e_dst[:, :], 7, None, ALU.arith_shift_right))
            v.tensor_copy(bk[:, :], ti[:, :])
            link(v.tensor_scalar(ti2[:, :], e_dst[:, :], P - 1, None, ALU.bitwise_and))
            v.tensor_copy(REC[:, :, 2].bitcast(F32), ti2[:, :])
            v.tensor_copy(REC[:, :, 0], e_src[:, :])
            link(v.tensor_copy(REC[:, :, 3].bitcast(F32), e_w[:, :]))
            v.scalar_tensor_tensor(out=REC[:, :, 1], in0=e_typ[:, :], scalar=float(NP), in1=e_src[:, :],
                                   op0=ALU.mult, op1=ALU.add)
            for b in range(NT):
                ins = v.tensor_scalar(oh[:, b, :], bk[:, :], float(b), None, ALU.is_equal)
            link(ins)
            for b in range(NT):
                ins = v.tensor_tensor_scan(run[:, b, :], oh[:, b, :], scan_zero[:, :], 0.0, ALU.add, ALU.add)
            ins.then_inc(tot_made, 1)
            v.wait_ge(pre_made, 1)
            link(v.tensor_scalar(basei[:, :], ps[:, 7, NT:2 * NT], float(P - 1), None, ALU.add))
            link(v.tensor_scalar(basei[:, :], basei[:, :], 7, None, ALU.arith_shift_right))
            link(v.tensor_copy(base[:, 0, :], basei[:, :]))
            link(v.memset(base[:, 3, :], 0.0))
            link(v.tensor_tensor_scan(base[:, 1, :], base[:, 0, :], base[:, 3, :], 0.0, ALU.add, ALU.add))
            link(v.tensor_tensor(base[:, 2, :], base[:, 1, :], base[:, 0, :], ALU.subtract))
            link(v.tensor_scalar(base[:, 2, :], base[:, 2, :], float(P), -1.0, ALU.mult, ALU.add))
            ins = v.tensor_tensor(base[:, 3, :], base[:, 2, :], ps[:, 7, 0:NT], ALU.add)
            link(ins)
            v.sem_inc(pre_read, 1)
            for b in range(NT):
                ins = v.scalar_tensor_tensor(out=run[:, b, :], in0=run[:, b, :], scalar=base[0:EP, 3, b:b + 1],
                                             in1=oh[:, b, :], op0=ALU.add, op1=ALU.mult)
            link(ins)
            link(v.tensor_reduce(slot[:, :], run[:, :, :].rearrange("p b c -> p c b"), AX_X, ALU.add))
            link(v.tensor_copy(ti[:, :], slot[:, :]))
            v.tensor_scalar(ti2[:, :], ti[:, :], P - 1, None, ALU.bitwise_and)
            link(v.tensor_scalar(ti[:, :], ti[:, :], 7, None, ALU.arith_shift_right))
            v.scalar_tensor_tensor(out=REC[:, :, 4], in0=ti2[:, :], scalar=float(TE), in1=ti[:, :],
                                   op0=ALU.mult, op1=ALU.add).then_inc(rec_made, 1)
            def tr_low(bank, to, n, count):
                v.wait_ge(tr_hi, count)
                v.tensor_tensor(to[:, LO, :, n * P:(n + 1) * P], ps[:, bank, :].rearrange("p (k m) -> p k m", k=KT),
                                to[:, HI, :, n * P:(n + 1) * P].bitcast(F32), ALU.subtract).then_inc(tr_out, 1)

            def w_low(j, count):
                v.wait_ge(w_hi, count)
                v.tensor_tensor(W[j % 2][:, LO, :, :], WS[j % 2][:, :, :], W[j % 2][:, HI, :, :].bitcast(F32),
                                ALU.subtract).then_inc(w_split, 1)

            tr_low(0, XT, 0, 1)
            w_low(0, 1)
            for n in range(1, NT):
                tr_low(n, XT, n, n + 1)
            v.wait_ge(consts, 6)
            link(v.tensor_scalar(tf[:, 0, :], iota_t[:, :], base[0:1, 1, 0:1], None, ALU.is_ge))
            for b in range(1, NT - 1):
                link(v.scalar_tensor_tensor(out=tf[:, b % 2, :], in0=iota_t[:, :], scalar=base[0:1, 1, b:b + 1],
                                            in1=tf[:, 1 - b % 2, :], op0=ALU.is_ge, op1=ALU.add))
            of_tile = tf[:, (NT - 2) % 2, :].rearrange("o (g m) -> o g m", m=PACK)
            word = tf[:, 1 - (NT - 2) % 2, 0:TE // PACK]
            link(v.tensor_copy(word, of_tile[:, :, 0]))
            for m in range(1, PACK):
                link(v.scalar_tensor_tensor(out=word, in0=of_tile[:, :, m], scalar=float(BASE ** m), in1=word,
                                            op0=ALU.mult, op1=ALU.add))
            v.tensor_copy(packed[:, :], word).then_inc(bucket_made, 1)

            v.wait_ge(small_in, 48)
            for t in range(NREL):
                ins = v.tensor_scalar(mask[:, t, :], nti[:, :], float(t), None, ALU.is_equal)
            link(v.tensor_scalar(eps1[:, :], eps1[:, :], 1.0, None, ALU.add))
            for t in range(NREL):
                v.wait_ge(row_in[3 + t], 16)
            for q in range(NREL * NT):
                r, n = divmod(q, NT)
                if n == 0:
                    w_low(r + 1, r + 2)
                v.wait_ge(prod_done, q + 1)
                v.wait_ge(row_in[r], 16)
                to = G[q][:, :] if q < RING else X[:, q - RING, :]
                v.tensor_tensor(to, ps[:, (5 + q) % 8, :], ROW[r][:, :], ALU.add).then_inc(prod_out, 1)
                if r == 0:
                    link(v.tensor_scalar(H[:, n, :], ROW[3][:, :], mask[:, 0, n:n + 1], None, ALU.mult))
                else:
                    link(v.scalar_tensor_tensor(out=H[:, n, :], in0=ROW[3 + r][:, :], scalar=mask[:, r, n:n + 1],
                                                in1=H[:, n, :], op0=ALU.mult, op1=ALU.add))
            for q in range(NREL * NT, 2 * NREL * NT):
                t, n = divmod(q - NREL * NT, NT)
                if n == 0 and t < NREL - 1:
                    w_low(NREL + t + 1, NREL + t + 2)
                v.wait_ge(prod_done, q + 1)
                if t:
                    v.wait_ge(prod_out, q - NT + 1)
                v.scalar_tensor_tensor(out=H[:, n, :], in0=ps[:, (5 + q) % 8, :], scalar=mask[:, t, n:n + 1],
                                       in1=H[:, n, :], op0=ALU.mult, op1=ALU.add).then_inc(prod_out, 1)

            v.wait_ge(rec_in, 16)
            link(v.tensor_copy(srcf[:, :], RS[:, :, 0]))
            dl = RS[:, :, 2].bitcast(F32)
            wt = RS[:, :, 3].bitcast(F32)
            v.sem_inc(oh_used, OR)
            with v.Fori(0, PASSES) as i:
                for k in range(RING):
                    v.wait_ge(oh_used, i * RING + k + 1)
                    v.tensor_scalar(SB[k % OR][:, :], iota_h[:, 0:P], dl[:, bass.ds(i * RING + k, 1)], None,
                                    ALU.is_equal)
                    v.tensor_scalar(OS[k % OR][:, :], iota_h[:, :], srcf[:, bass.ds(i * RING + k, 1)], None,
                                    ALU.is_equal).then_inc(oh_made, 1)
            v.wait_ge(cnt_out, 2 * NT)
            link(v.tensor_tensor(rstd[:, :], deg[:, 0, :], deg[:, 1, :], ALU.add))
            link(v.tensor_scalar(rstd[:, :], rstd[:, :], 1.0, None, ALU.max))
            v.reciprocal(rstd[:, :], rstd[:, :]).then_inc(deg_made, 1)

            def adj_low(a):
                v.wait_ge(adj_hi, a + 1)
                to, of = adj_part(LO, a)
                v.tensor_tensor(to, of, adj_part(HI, a)[0].bitcast(F32), ALU.subtract).then_inc(adj_out, 1)

            v.sem_inc(z_free, ZR)
            with v.Fori(0, PASSES) as i:
                for k in range(RING):
                    v.wait_ge(ring_free, i * RING + k + 1 + RING - ZR)
                    v.tensor_scalar(S[k % ZR][:, :], iota_f[:, :], dl[:, bass.ds(i * RING + k, 1)], None,
                                    ALU.is_equal).then_inc(s_made, 1)

            def stats(rows, n):
                link(v.bn_stats(st[:, n, 0, :], rows))
                v.sem_inc(dve_step, 1)
                v.bn_aggr(mv[:, n, :], st[:, n, 0, :]).then_inc(ln_var, 1)

            def normed(to, rows, n, ln_count):
                v.wait_ge(ln_sd, ln_count)
                link(v.reciprocal(rstd[:, n:n + 1], sd[:, n:n + 1]))
                return v.tensor_scalar(to, rows, mv[:, n, 0:1], rstd[:, n:n + 1], ALU.subtract, ALU.mult)

            def first_x(n):
                v.wait_ge(adj_tr, n + 1)
                normed(X[:, n, :], H[:, n, :], n, n + 1).then_inc(x_made, 1)

            for n in range(NT):
                v.wait_ge(acc_done, n + 1)
                link(v.tensor_tensor(H[:, n, :], ps[:, n, :], H[:, n, :], ALU.add))
                link(v.scalar_tensor_tensor(out=H[:, n, :], in0=H[:, n, :], scalar=0.0, in1=B[:, n, :],
                                            op0=ALU.max, op1=ALU.add))
                stats(H[:, n, :], n)
                if n:
                    first_x(n - 1)
                adj_low(n)
            first_x(NT - 1)
            for a in range(NT, TRJOBS):
                adj_low(a)

            def mean_parts(tr, agg, w):
                for n in range(NT):
                    tr_low((2 + n) % 5, XT, n, tr + n + 1)
                w_low(0, w + 1)
                w_low(1, w + 2)
                for a in range(2 * KT):
                    f, hf = divmod(a, 2)
                    v.wait_ge(agg_hi, agg + a + 1)
                    v.tensor_tensor(GT[:, LO, f, hf * HALF:(hf + 1) * HALF],
                                    ps[:, (5, 6, 7, 2, 3, 4, 0, 1)[a], 0:HALF],
                                    GT[:, HI, f, hf * HALF:(hf + 1) * HALF].bitcast(F32),
                                    ALU.subtract).then_inc(agg_out, 1)

            v.wait_ge(b_made, NT)

            def layer_stats(l, n):
                v.wait_ge(prod_done, l * NT + 2 * NREL * NT + n + 1)
                if n == 0:
                    for i in range(3):
                        v.wait_ge(row_in[i], l * 16 + 32)
                link(v.tensor_tensor(H[:, n, :], ps[:, (5, 6, 7, 0, 1)[n], :], ROW[0][:, :], ALU.add))
                stats(H[:, n, :], n)

            def layer_norm(n, ln_count):
                link(normed(H[:, n, :], H[:, n, :], n, ln_count))
                link(v.tensor_tensor(H[:, n, :], H[:, n, :], ROW[1][:, :], ALU.mult))
                link(v.tensor_tensor(H[:, n, :], H[:, n, :], ROW[2][:, :], ALU.add))
                v.scalar_tensor_tensor(out=X[:, n, :], in0=H[:, n, :], scalar=0.0, in1=X[:, n, :],
                                       op0=ALU.max, op1=ALU.add).then_inc(x_made, 1)

            PER1 = 6 * NT
            with v.Fori(0, NL1 - 1) as l:
                chain.enter(l * PER1)
                mean_parts(l * NT + NT, l * (2 * KT), l * 2 + 6)
                for n in range(NT):
                    layer_stats(l, n)
                    layer_norm(n, l * NT + NT + n + 1)
                chain.leave(PER1, NL1 - 1)
            l = NL1 - 1
            mean_parts(l * NT + NT, l * (2 * KT), l * 2 + 6)
            v.wait_ge(row_in[4], 32)
            for n in range(NT + 1):
                if n < NT:
                    layer_stats(l, n)
                if n:
                    v.wait_ge(sum_made, n)
                    stats(H[:, n - 1, :], n - 1)
                if n < NT:
                    layer_norm(n, NL1 * NT + LAST_L[n])
                if n:
                    normed(X[:, n - 1, :], H[:, n - 1, :], n - 1, NL1 * NT + LAST_E[n - 1]).then_inc(x_made, 1)
                    v.wait_ge(x_made, NL1 * NT + LAST_E[n - 1])
                    v.tensor_tensor(H[:, n - 1, :], X[:, n - 1, :], ROW[4][:, :], ALU.add).then_inc(xp_made, 1)

            X2 = NT + NL1 * NT + NT
            T2 = NT + NL1 * NT
            v.wait_ge(b_made, 2 * NT)
            PER2 = 6 * KT + NT
            with v.Fori(0, NL2) as l:
                chain.enter(l * PER2)
                v.tensor_copy(lcol[:, :, :], colt[:, :, bass.ds(l, 1), :].rearrange("p a o k -> p a (o k)"))\
                    .then_inc(lcol_made, 1)
                v.wait_ge(we_ok, l + 1)
                v.sem_inc(dve_step, 1)
                w_low(0, l * 2 + 13)
                w_low(1, l * 2 + 14)
                v.wait_ge(w_split, l * 2 + 14)
                v.sem_inc(dve_step, 1)
                with v.Fori(0, PASSES) as i:
                    for k in range(RING):
                        v.wait_ge(z_free, (l * PASSES + i) * RING + k + 1)
                        v.tensor_scalar(S[k % ZR][:, :], iota_f[:, :], dl[:, bass.ds(i * RING + k, 1)], None,
                                        ALU.is_equal).then_inc(s_made, 1)
                        v.wait_ge(gath[k], (l * PASSES + i + PASSES) * 16 + 16)
                        v.scalar_tensor_tensor(out=Z[:, k % ZR, :], in0=we_psum,
                                               scalar=wt[:, bass.ds(i * RING + k, 1)], in1=G[k][:, :],
                                               op0=ALU.mult, op1=ALU.add).then_inc(ring_free, 1)
                v.wait_ge(x_made, l * NT + X2)

                def g(n):
                    v.wait_ge(acc_done, l * NT + NT + n + 1)
                    v.scalar_tensor_tensor(out=H[:, n, :], in0=X[:, n, :], scalar=eps1[:, bass.ds(l, 1)],
                                           in1=ps[:, n, :], op0=ALU.mult, op1=ALU.add).then_inc(g_made, 1)

                for n in range(NT + 2):
                    if n < NT:
                        g(n)
                    if n >= 2:
                        tr_low(n - 2, GT, n - 2, l * NT + T2 + n - 1)

                def h_stats(o, hf):
                    v.wait_ge(ht_raw, l * (2 * KT) + HJOBS.index((o, hf)) + 1)
                    link(v.bn_stats(st[:, o, hf, :], HR[:, o, 0:HALF] if hf == 0 else HR[:, o, HALF:N]))

                def h_norm(o):
                    v.wait_ge(bn_sd, l * KT + o + 1)
                    link(v.reciprocal(rstd[:, o:o + 1], sd[:, o:o + 1]))
                    link(v.tensor_tensor(sc[:, 0, o:o + 1], rstd[:, o:o + 1], lcol[:, 1, o:o + 1], ALU.mult))
                    link(v.tensor_tensor(msc[:, o:o + 1], mv[:, o, 0:1], sc[:, 0, o:o + 1], ALU.mult))
                    link(v.tensor_tensor(sc[:, 1, o:o + 1], lcol[:, 2, o:o + 1], msc[:, o:o + 1], ALU.subtract))
                    v.tensor_scalar(HR[:, o, :], HR[:, o, :], sc[:, 0, o:o + 1], sc[:, 1, o:o + 1], ALU.mult,
                                    ALU.add).then_inc(ht_norm, 1)

                def h_low(o):
                    v.wait_ge(ht_hi, l * KT + o + 1)
                    v.scalar_tensor_tensor(out=XT[:, LO, o, :], in0=HR[:, o, :], scalar=0.0,
                                           in1=XT[:, HI, o, :].bitcast(F32), op0=ALU.max,
                                           op1=ALU.subtract).then_inc(ht_out, 1)

                for o in range(KT):
                    h_stats(o, 0)
                    if o:
                        h_norm(o - 1)
                    h_stats(o, 1)
                    v.sem_inc(dve_step, 1)
                    v.bn_aggr(mv[:, o, :], st[:, o, :, :].rearrange("p a s -> p (a s)")).then_inc(bn_var, 1)
                    if o:
                        h_low(o - 1)
                h_norm(KT - 1)
                h_low(KT - 1)
                v.wait_ge(row_in[5], l * 16 + 32)
                v.wait_ge(row_in[4], l * 16 + 48)
                for n in range(NT):
                    v.wait_ge(prod_done, l * NT + (2 * NREL + NL1) * NT + n + 1)
                    link(v.tensor_tensor(X[:, n, :], ps[:, n, :], ROW[5][:, :], ALU.add))
                    v.scalar_tensor_tensor(out=H[:, n, :], in0=X[:, n, :], scalar=0.0, in1=ROW[4][:, :],
                                           op0=ALU.max, op1=ALU.add).then_inc(xp_made, 1)
                chain.leave(PER2, NL2)
            for n in range(NT + 1):
                if n < NT:
                    v.wait_ge(sum_made, NT + n + 1)
                    stats(H[:, n, :], n)
                if n:
                    normed(X[:, n - 1, :], H[:, n - 1, :], n - 1, X2 + n).then_inc(x_made, 1)

            mean_parts(T2 + NL2 * NT, NL1 * 2 * KT, 20)
            v.wait_ge(row_in[0], 16 * (NL1 + 2))
            v.wait_ge(b_made, 3 * NT)
            PR3 = (2 * NREL + NL1 + NL2) * NT
            for n in range(NT):
                v.wait_ge(prod_done, PR3 + n + 1)
                v.tensor_tensor(H[:, n, :], ps[:, (5, 6, 7, 0, 1)[n], :], ROW[0][:, :], ALU.add).then_inc(sg_in, 1)
                v.wait_ge(sg_out, n + 1)
                link(v.tensor_tensor(X[:, n, :], X[:, n, :], H[:, n, :], ALU.mult))
                link(v.tensor_tensor(X[:, n, :], X[:, n, :], B[:, n, :], ALU.add))
                stats(X[:, n, :], n)
            for n in range(NT):
                normed(H[:, n, :], X[:, n, :], n, NT + NL1 * NT + NT + NT + n + 1).then_inc(o_made, 1)


def kernel(**inputs):
    import concourse.bacc as _bacc
    from concourse.bass_utils import run_bass_kernel_spmd as _run

    a = {k: np.asarray(v) for k, v in inputs.items()}
    nodes = np.pad(a["node_type_3"], (0, NP - N)).reshape(NT, P).T
    cols = np.stack([a["L2_gnn_" + c].reshape(NL2, KT, P).transpose(2, 0, 1) for c in ("b1", "gamma", "beta")],
                    axis=1)
    again = lambda r: np.concatenate([r, r[:1]])
    pairs = [(a["L1_gnn_W_r"][i].T, a["L1_gnn_W_l"][i].T) for i in range(NL1)]
    pairs += [(a["L2_gnn_W1"][i], a["L2_gnn_W2"][i]) for i in range(NL2)]
    pairs += [(a["L3_gnn_W_r"], a["L3_gnn_W_l"])]
    weights = np.stack([*a["L0_gnn_W_rel"], *a["L0_gnn_W_self"], *(w for p in pairs for w in p)])
    given = {
        "x": a["x"], "src": a["src"].reshape(EP, EC), "dst": a["dst"].reshape(EP, EC),
        "etype": a["edge_type_3"].reshape(EP, EC), "ew": a["edge_weight1"].reshape(EP, EC), "ntype": nodes,
        "weights": weights, "b_rel": a["L0_gnn_b_rel"], "b_self": a["L0_gnn_b_self"],
        "b1_l1": a["L1_gnn_b"], "ln_g": a["L1_gnn_ln_g"], "ln_b": a["L1_gnn_ln_b"],
        "eps": a["L2_gnn_eps"].reshape(1, NL2), "we": again(a["L2_gnn_We"].reshape(NL2, D)),
        "be": again(a["L2_gnn_be"]), "cols": cols,
        "b2": a["L2_gnn_b2"], "b3": a["L3_gnn_b"].reshape(1, D),
    }
    nc = _bacc.Bacc("TRN2", target_bir_lowering=False, num_devices=1)
    arrays, args = {}, []
    for name, v in given.items():
        arrays[f"in_{name}"] = np.ascontiguousarray(v)
        args.append(nc.dram_tensor(f"in_{name}", v.shape, mybir.dt.from_np(v.dtype), kind="ExternalInput").ap())
    args.append(nc.dram_tensor("out_0", (N, D), F32, kind="ExternalOutput").ap())
    build(nc, *args)
    return _run(nc, [arrays], core_ids=[0]).results[0]["out_0"]
```
